# Optimizing a Trainium2 kernel written in Bass

```python
import numpy as np
import jax
import jax.numpy as jnp

def _softmax(x, axis=-1):
    return jax.nn.softmax(x, axis=axis)

def _gelu(x):
    return jax.nn.gelu(x, approximate=True)

def _silu(x):
    return jax.nn.silu(x)

def _sigmoid(x):
    return jax.nn.sigmoid(x)

def _layernorm(x, axis=-1, eps=1e-05):
    m = jnp.mean(x, axis=axis, keepdims=True)
    v = jnp.var(x, axis=axis, keepdims=True)
    return (x - m) / jnp.sqrt(v + eps)

def _scatter_add(tgt, idx, src, axis=0):
    return tgt.at[idx].add(src)

def _segment_sum(src, seg, n):
    return jax.ops.segment_sum(src, seg, n)
kernel_name = 'mk_prb_d1_jaxref_r4_905203'

def setup_inputs(seed: int=0):
    np.random.seed(seed)
    _w = jnp.asarray

    def _L0_attn_setup():
        import jax, jax.numpy as jnp
        import numpy as np
        H = 16
        D_H = 128
        D_HR = 64
        THETA = 10000.0

        def rope(x, pos, theta=THETA):
            d = x.shape[-1]
            inv_freq = theta ** (-jnp.arange(0, d, 2, dtype=jnp.float32) / d)
            ang = pos.astype(jnp.float32)[:, None] * inv_freq[None, :]
            cos, sin = (jnp.cos(ang), jnp.sin(ang))
            x1, x2 = (x[..., 0::2], x[..., 1::2])
            out = jnp.stack([x1 * cos - x2 * sin, x1 * sin + x2 * cos], axis=-1)
            return out.reshape(x.shape)
        key = jax.random.key(seed)
        ks = jax.random.split(key, 9)
        d_model, d_latent = (512, 128)

        def w(k, shape):
            fan_in = shape[-1]
            return jax.random.normal(k, shape, dtype=jnp.float32) / jnp.sqrt(fan_in)
        return {'x': jax.random.normal(ks[0], (1, 512, d_model), dtype=jnp.float32), 'W_DQ': w(ks[1], (d_latent, d_model)), 'W_UQ': w(ks[2], (H * D_H, d_latent)), 'W_QR': w(ks[3], (H * D_HR, d_latent)), 'W_DKV': w(ks[4], (d_latent, d_model)), 'W_UK': w(ks[5], (H * D_H, d_latent)), 'W_UV': w(ks[6], (H * D_H, d_latent)), 'W_KR': w(ks[7], (D_HR, d_model)), 'W_O': w(ks[8], (d_model, H * D_H))}
    _L0_attn_in = _L0_attn_setup()

    def _L0_ffn_setup():
        import jax, jax.numpy as jnp
        import numpy as np
        NUM_ROUTED = 7
        TOP_K = 3
        D = 512
        H = 512
        B, S = (4, 512)

        def _expert_ffn(x, w1, wg, w2):
            return jax.nn.silu(x @ w1) * (x @ wg) @ w2
        key = jax.random.key(seed)
        ks = jax.random.split(key, 8)
        s = 0.02
        return {'x': jax.random.normal(ks[0], (B, S, D), jnp.float32), 'W1': jax.random.normal(ks[1], (NUM_ROUTED, D, H), jnp.float32) * s, 'Wg': jax.random.normal(ks[2], (NUM_ROUTED, D, H), jnp.float32) * s, 'W2': jax.random.normal(ks[3], (NUM_ROUTED, H, D), jnp.float32) * s, 'Ws1': jax.random.normal(ks[4], (D, H), jnp.float32) * s, 'Wsg': jax.random.normal(ks[5], (D, H), jnp.float32) * s, 'Ws2': jax.random.normal(ks[6], (H, D), jnp.float32) * s, 'gate_w': jax.random.normal(ks[7], (D, NUM_ROUTED), jnp.float32) * s, 'gate_b': jnp.zeros((NUM_ROUTED,), jnp.float32), 'biases': jnp.zeros((NUM_ROUTED,), jnp.float32)}
    _L0_ffn_in = _L0_ffn_setup()
    _d = {'L0_attn_x': _L0_attn_in['x'], 'L0_attn_W_DQ': _L0_attn_in['W_DQ'], 'L0_attn_W_UQ': _L0_attn_in['W_UQ'], 'L0_attn_W_QR': _L0_attn_in['W_QR'], 'L0_attn_W_DKV': _L0_attn_in['W_DKV'], 'L0_attn_W_UK': _L0_attn_in['W_UK'], 'L0_attn_W_UV': _L0_attn_in['W_UV'], 'L0_attn_W_KR': _L0_attn_in['W_KR'], 'L0_attn_W_O': _L0_attn_in['W_O'], 'L0_ffn_W1': _L0_ffn_in['W1'], 'L0_ffn_Wg': _L0_ffn_in['Wg'], 'L0_ffn_W2': _L0_ffn_in['W2'], 'L0_ffn_Ws1': _L0_ffn_in['Ws1'], 'L0_ffn_Wsg': _L0_ffn_in['Wsg'], 'L0_ffn_Ws2': _L0_ffn_in['Ws2'], 'L0_ffn_gate_w': _L0_ffn_in['gate_w'], 'L0_ffn_gate_b': _L0_ffn_in['gate_b'], 'L0_ffn_biases': _L0_ffn_in['biases']}
    _x0 = _d['L0_attn_x']
    _d['L0_attn_x'] = jax.random.normal(jax.random.fold_in(jax.random.key(seed), 1), (4, 512, 512), dtype=_x0.dtype)
    del _x0
    return _d

def reference(L0_attn_x, L0_attn_W_DQ, L0_attn_W_UQ, L0_attn_W_QR, L0_attn_W_DKV, L0_attn_W_UK, L0_attn_W_UV, L0_attn_W_KR, L0_attn_W_O, L0_ffn_W1, L0_ffn_Wg, L0_ffn_W2, L0_ffn_Ws1, L0_ffn_Wsg, L0_ffn_Ws2, L0_ffn_gate_w, L0_ffn_gate_b, L0_ffn_biases):

    def _L0_attn_ref(x, W_DQ, W_UQ, W_QR, W_DKV, W_UK, W_UV, W_KR, W_O):
        import jax, jax.numpy as jnp
        import numpy as np
        H = 16
        D_H = 128
        D_HR = 64
        THETA = 10000.0

        def rope(x, pos, theta=THETA):
            d = x.shape[-1]
            inv_freq = theta ** (-jnp.arange(0, d, 2, dtype=jnp.float32) / d)
            ang = pos.astype(jnp.float32)[:, None] * inv_freq[None, :]
            cos, sin = (jnp.cos(ang), jnp.sin(ang))
            x1, x2 = (x[..., 0::2], x[..., 1::2])
            out = jnp.stack([x1 * cos - x2 * sin, x1 * sin + x2 * cos], axis=-1)
            return out.reshape(x.shape)
        B, S, _ = x.shape
        pos = jnp.arange(S)
        c_Q = x @ W_DQ.T
        q_C = (c_Q @ W_UQ.T).reshape(B, S, H, D_H).transpose(0, 2, 1, 3)
        q_R = (c_Q @ W_QR.T).reshape(B, S, H, D_HR).transpose(0, 2, 1, 3)
        q_R = rope(q_R, pos)
        q = jnp.concatenate([q_C, q_R], axis=-1)
        c_KV = x @ W_DKV.T
        k_C = (c_KV @ W_UK.T).reshape(B, S, H, D_H).transpose(0, 2, 1, 3)
        k_R = rope(x @ W_KR.T, pos)[:, None]
        k_R = jnp.broadcast_to(k_R, (B, H, S, D_HR))
        k = jnp.concatenate([k_C, k_R], axis=-1)
        v = (c_KV @ W_UV.T).reshape(B, S, H, D_H).transpose(0, 2, 1, 3)
        d_qk = D_H + D_HR
        scores = jnp.einsum('bhqd,bhkd->bhqk', q, k)
        scores = jnp.clip(scores, -80.0, 80.0)
        causal = pos[:, None] >= pos[None, :]
        scores = jnp.where(causal[None, None], scores, -jnp.inf)
        weights = jax.nn.softmax(scores / jnp.sqrt(jnp.float32(d_qk)), axis=-1)
        attn = jnp.einsum('bhqk,bhkd->bhqd', weights, v)
        out = attn.transpose(0, 2, 1, 3).reshape(B, S, H * D_H) @ W_O.T
        return out

    def _L0_ffn_ref(x, W1, Wg, W2, Ws1, Wsg, Ws2, gate_w, gate_b, biases):
        import jax, jax.numpy as jnp
        import numpy as np
        NUM_ROUTED = 7
        TOP_K = 3
        D = 512
        H = 512
        B, S = (4, 512)

        def _expert_ffn(x, w1, wg, w2):
            return jax.nn.silu(x @ w1) * (x @ wg) @ w2
        output = _expert_ffn(x, Ws1, Wsg, Ws2)
        gate_logits = x @ gate_w + gate_b
        gate_probas = jax.nn.softmax(gate_logits, axis=-1)
        biased_probas = gate_probas + biases
        _, topk_idxs = jax.lax.top_k(biased_probas, TOP_K)
        topk_probas = jnp.take_along_axis(gate_probas, topk_idxs, axis=-1)
        topk_probas = topk_probas / jnp.sum(topk_probas, axis=-1, keepdims=True)
        for e in range(NUM_ROUTED):
            w_e = jnp.sum(topk_probas * (topk_idxs == e), axis=-1)
            output = output + _expert_ffn(x, W1[e], Wg[e], W2[e]) * w_e[..., None]
        return output
    x = L0_attn_x
    xn = _layernorm(x, axis=-1)
    x = x + _L0_attn_ref(xn, L0_attn_W_DQ, L0_attn_W_UQ, L0_attn_W_QR, L0_attn_W_DKV, L0_attn_W_UK, L0_attn_W_UV, L0_attn_W_KR, L0_attn_W_O) + _L0_ffn_ref(xn, L0_ffn_W1, L0_ffn_Wg, L0_ffn_W2, L0_ffn_Ws1, L0_ffn_Wsg, L0_ffn_Ws2, L0_ffn_gate_w, L0_ffn_gate_b, L0_ffn_biases)
    return x

_drawn_inputs = setup_inputs


def setup_inputs(seed=0):
    import zlib

    import numpy as np

    out = dict(_drawn_inputs(seed))
    spreads = {'L0_ffn_gate_b': (0.0, 2.0), 'L0_ffn_biases': (0.0, 1.244)}
    factors = {'L0_ffn_gate_w': 8.44}
    for name, (base, spread) in spreads.items():
        noise = np.random.default_rng([zlib.crc32(name.encode()), seed]).standard_normal(out[name].shape)
        drawn = base * np.exp(spread * noise) if base else spread * noise
        out[name] = jnp.asarray(drawn.astype(out[name].dtype))
    for name, factor in factors.items():
        out[name] = (out[name] * factor).astype(out[name].dtype)
    return out
```

```python
from contextlib import ExitStack

import numpy as np

import concourse.bass as bass
from concourse import mybir

ALU = mybir.AluOpType
ACT = mybir.ActivationFunctionType
AX = mybir.AxisListType
F32 = mybir.dt.float32
F32R = mybir.dt.float32r

P = 128
BANK = 512
LN_EPS = 1e-5
TOP_K = 3
CLIP = 80.0


class Ticket:

    def __init__(self, sem, value):
        self.sem, self.value = sem, value


class Queue:

    def __init__(self, sem):
        self.sem, self.steps, self.count, self.waited = sem, [], 0, {}

    def wait(self, *tickets):
        for t in tickets:
            if t is None or self.waited.get(id(t.sem), 0) >= t.value:
                continue
            self.waited[id(t.sem)] = t.value
            self.steps.append(lambda eng, t=t: eng.wait_ge(t.sem, t.value))

    def do(self, make):
        self.count += 1
        self.steps.append(lambda eng: make(eng).then_inc(self.sem, 1))
        return Ticket(self.sem, self.count)

    def quiet(self, make):
        self.steps.append(lambda eng: make(eng))

    def run(self, eng):
        for step in self.steps:
            step(eng)


class Stream:

    def __init__(self, sem):
        self.sem, self.count = sem, 0

    def start(self, queue, out, in_):
        self.count += 16
        queue.steps.append(lambda eng: eng.dma_start(out, in_).then_inc(self.sem, 16))
        return Ticket(self.sem, self.count)


class Slot:

    def __init__(self, ap):
        self.ap, self.free, self.ready = ap, [], []


class Ring:
    def __init__(self, slots):
        self.slots, self.at = slots, 0

    def next(self):
        s = self.slots[self.at % len(self.slots)]
        self.at += 1
        return s


def product(pe, out, pairs, first=True, last=True):
    t = None
    for n, (a, b) in enumerate(pairs):
        start, stop = first and n == 0, last and n == len(pairs) - 1
        make = lambda eng, a=a, b=b, start=start, stop=stop: eng.matmul(out, a, b, start=start, stop=stop)
        if n == len(pairs) - 1:
            t = pe.do(make)
        else:
            pe.quiet(make)
    return t


def split3(a_hi, a_lo, b_hi, b_lo):
    return [(a_hi, b_hi), (a_hi, b_lo), (a_lo, b_hi)]


def program(nc, x, wdqt, wuq, wqrt, wdkvt, wuk, wuv, wkrt, wot, w1, wg, w2, ws1, wsg, ws2,
            gate_w, gate_b, biases, rope_cos, rope_sin, out):
    BATCH, SEQ, D = x.shape
    TOK = BATCH * SEQ
    NT = TOK // P
    NB = TOK // BANK
    TB = BANK // P
    NE, _, HID = w1.shape
    DC, HC = D // P, HID // P
    LAT = wdqt.shape[1]
    DR = wkrt.shape[1]
    HEADS = wuq.shape[0] // P
    PAIRS = HEADS // 2
    DH = wuq.shape[0] // HEADS
    SCALE = float(1.0 / np.sqrt(np.float32(DH + DR)))
    assert SEQ == BANK and LAT == P and 2 * DR == P and DH == P and D == BANK

    x_t = x.rearrange("b (t p) d -> p (b t) d", p=P)
    out_t = out.rearrange("b (t p) d -> p (b t) d", p=P)

    with ExitStack() as whole:
        def tile(ctx, name, shape, dt=F32):
            return ctx.enter_context(nc.sbuf_tensor(name, shape, dt))

        def sem(ctx, name):
            return ctx.enter_context(nc.semaphore(name))

        def queues(ctx, tag):
            return [Queue(sem(ctx, f"{tag}_{n}_done")) for n in ("pe", "act", "dve", "pool")]

        banks = [whole.enter_context(nc.psum_tensor(f"bank{i}", [P, BANK], F32)) for i in range(5)]
        score_banks = whole.enter_context(nc.psum_tensor("score_banks", [P, 3, BANK], F32))

        acc = tile(whole, "acc", [P, NT, D])
        store_a = tile(whole, "store_a", [P, 16384], F32R)
        store_b = tile(whole, "store_b", [P, 16384], F32R)
        ident = tile(whole, "ident", [P, P])

        xnt = store_b[:].rearrange("p (s c t) -> p s c t", s=2, c=DC)
        xnt_hi, xnt_lo = xnt[:, 0], xnt[:, 1]

        with ExitStack() as ctx:
            pe, act, dve, pool = queues(ctx, "ffn")
            sp, act_dma = Queue(None), act

            UPS, DNS = 5, 6
            up_w = store_a[:, 0:UPS * 2048].rearrange("p (n s m c h) -> p n s m c h", n=UPS, s=2, m=2, c=DC)
            dn_w = store_a[:, UPS * 2048:UPS * 2048 + DNS * 1024].rearrange("p (n s d) -> p n s d", n=DNS, s=2)
            up_slots = [Slot(up_w[:, n]) for n in range(UPS)]
            dn_slots = [Slot(dn_w[:, n]) for n in range(DNS)]
            raw_up = tile(ctx, "raw_up", [P, 2, 2, DC, P])
            raw_dn = tile(ctx, "raw_dn", [P, 2, D])
            g_store = tile(ctx, "g_store", [P, 2, 2, BANK], F32R)
            s_store = tile(ctx, "s_store", [P, 2, BANK])
            h_store = tile(ctx, "h_store", [P, 2, BANK])
            stats = tile(ctx, "stats", [P, NT, 6])
            mv = tile(ctx, "mv", [P, NT, 2])
            var_eps = tile(ctx, "var_eps", [P, NT])
            rstd = tile(ctx, "rstd", [P, NT])
            neg_half = tile(ctx, "neg_half", [P, NT])
            gw_raw = tile(ctx, "gw_raw", [P, DC, 8])
            gw = tile(ctx, "gw", [P, DC, 16], F32R)
            gb = tile(ctx, "gb", [P, 8])
            eb = tile(ctx, "eb", [P, 8])
            logit = tile(ctx, "logit", [P, NT, 8])
            prob = tile(ctx, "prob", [P, NT, 8])
            biased = tile(ctx, "biased", [P, NT, 8])
            beats = tile(ctx, "beats", [P, NT, 8])
            rank = tile(ctx, "rank", [P, NT, 8])
            chosen = tile(ctx, "chosen", [P, NT, 8])
            share = tile(ctx, "share", [P, NT, 8])
            col = tile(ctx, "col", [P, NT, 2])

            x_in = [Stream(sem(ctx, f"x_in{b}")) for b in range(NB)]
            gate_in = Stream(sem(ctx, "gate_in"))
            wu_in = [Stream(sem(ctx, f"wu_in{n}")) for n in range(2)]
            wg_in = [Stream(sem(ctx, f"wg_in{n}")) for n in range(2)]
            wd_in = [Stream(sem(ctx, f"wd_in{n}")) for n in range(2)]

            x_here = [x_in[b].start(sp, acc[:, b * TB:(b + 1) * TB, :], x_t[:, b * TB:(b + 1) * TB, :])
                      for b in range(NB)]

            t = pool.do(lambda e: e.memset(ident[:], 0.0))
            pool.wait(t)
            ident_made = pool.do(lambda e: e.affine_select(
                out=ident[:], in_=ident[:], compare_op=ALU.not_equal, fill=1.0, base=0,
                pattern=[[-1, P]], channel_multiplier=1))
            half_made = pool.do(lambda e: e.memset(neg_half[:], -0.5))
            pad_made = pool.do(lambda e: e.memset(gw_raw[:], 0.0))

            up_ring = Ring([Slot(b[:]) for b in banks[0:4]])
            y_slots = [Slot(banks[4][:])] + [Slot(score_banks[:, i, :]) for i in range(3)]
            xn_ring = Ring([Slot(s_store[:, i, :]) for i in range(2)])

            def layer_norm(b):
                tiles = range(b * TB, (b + 1) * TB)
                for t in tiles:
                    dve.wait(x_here[b])
                    dve.do(lambda e, t=t: e.bn_stats(out=stats[:, t, :], in_=acc[:, t, :]))
                for t in tiles:
                    dve.wait(Ticket(dve.sem, dve.count))
                    dve.do(lambda e, t=t: e.bn_aggr(out=mv[:, t, :], in_=stats[:, t, :]))
                dve.wait(Ticket(dve.sem, dve.count))
                var_ready = dve.do(lambda e: e.tensor_scalar(
                    var_eps[:, b * TB:(b + 1) * TB], mv[:, b * TB:(b + 1) * TB, 1], LN_EPS, None, ALU.add))
                pool.wait(var_ready, half_made)
                rstd_ready = pool.do(lambda e: e.tensor_tensor(
                    rstd[:, b * TB:(b + 1) * TB], var_eps[:, b * TB:(b + 1) * TB],
                    neg_half[:, b * TB:(b + 1) * TB], ALU.pow))
                dve.wait(rstd_ready)
                for t in tiles:
                    xn, bank = xn_ring.next(), up_ring.next()
                    dve.wait(*xn.free)
                    xn_ready = dve.do(lambda e, t=t, xn=xn: e.tensor_scalar(
                        xn.ap, acc[:, t, :], mv[:, t, 0:1], rstd[:, t:t + 1], ALU.subtract, ALU.mult))
                    pe.wait(xn_ready, ident_made, *bank.free)
                    for c in range(DC):
                        turn = (lambda e, c=c, xn=xn, bank=bank: e.transpose(
                            bank.ap[:, c * P:(c + 1) * P], xn.ap[:, c * P:(c + 1) * P], ident[:]))
                        if c < DC - 1:
                            pe.quiet(turn)
                    turned = pe.do(turn)
                    xn.free = [turned]
                    src = bank.ap.rearrange("p (c t) -> p c t", c=DC)
                    cols = slice(t * P, (t + 1) * P)
                    act.wait(turned)
                    hi = act.do(lambda e, src=src, cols=cols: e.activation(xnt_hi[:, :, cols], src, ACT.Copy))
                    dve.wait(hi)
                    lo = dve.do(lambda e, src=src, cols=cols: e.tensor_tensor(
                        xnt_lo[:, :, cols], src, xnt_hi[:, :, cols].bitcast(F32), ALU.subtract))
                    bank.free = [lo]
                return lo

            def load_weights(k):
                e, hc = divmod(k, HC)
                r = k % 2
                src1, srcg, src2 = (ws1, wsg, ws2) if e == 0 else (w1[e - 1], wg[e - 1], w2[e - 1])
                cols = slice(hc * P, (hc + 1) * P)
                sp.wait(*raw_free[r])
                a = wu_in[r].start(sp, raw_up[:, r, 0], src1.rearrange("(c p) h -> p c h", p=P)[:, :, cols])
                b = wg_in[r].start(sp, raw_up[:, r, 1], srcg.rearrange("(c p) h -> p c h", p=P)[:, :, cols])
                c = wd_in[r].start(sp, raw_dn[:, r], src2[cols, :])
                up, dn = up_slots[k % UPS], dn_slots[k % DNS]
                act.wait(a, b, *up.free)
                up_hi = act.do(lambda g: g.activation(up.ap[:, 0], raw_up[:, r], ACT.Copy))
                act.wait(c, *dn.free)
                dn_hi = act.do(lambda g: g.activation(dn.ap[:, 0], raw_dn[:, r], ACT.Copy))
                pool.wait(up_hi)
                up_lo = pool.do(lambda g: g.tensor_tensor(
                    up.ap[:, 1], raw_up[:, r], up.ap[:, 0].bitcast(F32), ALU.subtract))
                pool.wait(dn_hi)
                dn_lo = pool.do(lambda g: g.tensor_tensor(
                    dn.ap[:, 1], raw_dn[:, r], dn.ap[:, 0].bitcast(F32), ALU.subtract))
                raw_free[r] = [dn_lo]
                weights[k] = (up.ap, dn.ap, up_lo, dn_lo)

            raw_free = {0: [], 1: []}
            weights = {}
            g_ring = Ring([Slot(g_store[:, i]) for i in range(2)])
            s_ring = Ring([Slot(s_store[:, i, :]) for i in range(2)])
            h_ring = Ring([Slot(h_store[:, i, :]) for i in range(2)])

            def up(e, tb, hc, xnt_ready):
                k = e * HC + hc
                w, _, w_ready, _ = weights[k]
                toks = slice(tb * BANK, (tb + 1) * BANK)
                bank1, bankg = up_ring.next(), up_ring.next()
                done = []
                for m, bank in ((0, bank1), (1, bankg)):
                    pe.wait(w_ready, xnt_ready, *bank.free)
                    pairs = []
                    for c in range(DC):
                        pairs += split3(w[:, 0, m, c, :], w[:, 1, m, c, :],
                                        xnt_hi[:, c, toks], xnt_lo[:, c, toks])
                    done.append(product(pe, bank.ap, pairs))
                if tb == NB - 1:
                    up_slots[k % UPS].free = [done[1]]
                s, h, g = s_ring.next(), h_ring.next(), g_ring.next()
                act.wait(done[0], *s.free)
                s_ready = act.do(lambda q: q.activation(s.ap, bank1.ap, ACT.Silu))
                bank1.free = [s_ready]
                dve.wait(s_ready, done[1], *h.free)
                h_ready = dve.do(lambda q: q.tensor_tensor(h.ap, bankg.ap, s.ap, ALU.mult))
                bankg.free = [h_ready]
                s.free = [h_ready]
                act.wait(h_ready, *g.free)
                hi = act.do(lambda q: q.activation(g.ap[:, 0], h.ap, ACT.Copy))
                dve.wait(hi)
                lo = dve.do(lambda q: q.tensor_tensor(g.ap[:, 1], h.ap, g.ap[:, 0].bitcast(F32), ALU.subtract))
                h.free = [lo]
                return g, lo

            acc_done = {}

            def down(e, tb, hc, g, g_ready):
                k = e * HC + hc
                _, w, _, w_ready = weights[k]
                pe.wait(g_ready, w_ready)
                for tt in range(TB):
                    y = y_slots[tt]
                    if hc == 0:
                        pe.wait(*y.free)
                    cols = slice(tt * P, (tt + 1) * P)
                    done = product(pe, y.ap, split3(g.ap[:, 0, cols], g.ap[:, 1, cols], w[:, 0], w[:, 1]),
                                   first=hc == 0, last=hc == HC - 1)
                    if hc == HC - 1:
                        t = tb * TB + tt
                        dve.wait(done, acc_done.get(t))
                        if e == 0:
                            y_read = dve.do(lambda q, y=y, t=t: q.tensor_tensor(
                                acc[:, t, :], y.ap, acc[:, t, :], ALU.add))
                        else:
                            dve.wait(share_ready[0])
                            y_read = dve.do(lambda q, y=y, t=t: q.scalar_tensor_tensor(
                                acc[:, t, :], y.ap, share[:, t, e - 1:e], acc[:, t, :], ALU.mult, ALU.add))
                        y.free = [y_read]
                        acc_done[t] = y_read
                g.free = [done]
                if tb == NB - 1:
                    dn_slots[k % DNS].free = [done]

            share_ready = [None]

            def gate(xnt_ready):
                act.wait(gate_here[0])
                gw_hi = act.do(lambda q: q.activation(gw[:, :, 0:8], gw_raw[:], ACT.Copy))
                dve.wait(gw_hi)
                gw_lo = dve.do(lambda q: q.tensor_tensor(gw[:, :, 8:16], gw_raw[:], gw[:, :, 0:8].bitcast(F32),
                                                         ALU.subtract))
                back = up_ring.next()
                pe.wait(gw_lo, xnt_ready)
                for b in range(NB):
                    bank, rows = up_ring.next(), h_ring.next()
                    if bank is back:
                        bank = up_ring.next()
                    toks = slice(b * BANK, (b + 1) * BANK)
                    pe.wait(*bank.free)
                    product(pe, bank.ap[0:16, :], [(gw[:, c, :], xnt_hi[:, c, toks]) for c in range(DC)], last=False)
                    done = product(pe, bank.ap[0:8, :], [(gw[:, c, 0:8], xnt_lo[:, c, toks]) for c in range(DC)],
                                   first=False)
                    act.wait(done, *rows.free)
                    copied = act.do(lambda q, rows=rows, bank=bank: q.activation(
                        rows.ap[0:16, :], bank.ap[0:16, :], ACT.Copy))
                    bank.free = [copied]
                    pe.wait(copied, *back.free)
                    for t in range(TB):
                        turned = pe.do(lambda q, b=b, t=t, rows=rows: q.transpose(
                            back.ap[:, (b * TB + t) * 16:(b * TB + t + 1) * 16],
                            rows.ap[0:16, t * P:(t + 1) * P], ident[0:16, 0:16]))
                    rows.free = [turned]
                act.wait(turned)
                both = back.ap[:, 0:NT * 16].rearrange("p (t e) -> p t e", e=16)
                got = act.do(lambda q: q.activation(logit[:], both[:, :, 0:8], ACT.Copy))
                dve.wait(got)
                got = dve.do(lambda q: q.tensor_tensor(logit[:], both[:, :, 8:16], logit[:], ALU.add))
                back.free = [got]
                dve.wait(got)

                def chain(make):
                    t = dve.do(make)
                    dve.wait(t)
                    return t

                ex = slice(0, NE)

                def over(v):
                    return v.unsqueeze(1).broadcast_to([P, NT, NE])

                def spread(v):
                    return v.broadcast_to([P, NT, NE])

                chain(lambda q: q.tensor_tensor(logit[:, :, ex], logit[:, :, ex], over(gb[:, ex]), ALU.add))
                chain(lambda q: q.tensor_reduce(col[:, :, 0], logit[:, :, ex], AX.X, ALU.max))
                t = chain(lambda q: q.tensor_tensor(logit[:, :, ex], logit[:, :, ex], spread(col[:, :, 0:1]),
                                                    ALU.subtract))
                act.wait(t)
                t = act.do(lambda q: q.activation(prob[:, :, ex], logit[:, :, ex], ACT.Exp))
                dve.wait(t)
                chain(lambda q: q.tensor_reduce(col[:, :, 0], prob[:, :, ex], AX.X, ALU.add))
                chain(lambda q: q.reciprocal(col[:, :, 1], col[:, :, 0]))
                chain(lambda q: q.tensor_tensor(prob[:, :, ex], prob[:, :, ex], spread(col[:, :, 1:2]), ALU.mult))
                chain(lambda q: q.tensor_tensor(biased[:, :, ex], prob[:, :, ex], over(eb[:, ex]), ALU.add))
                for n in range(NE):
                    if n:
                        chain(lambda q, n=n: q.tensor_tensor(
                            beats[:, :, 0:n], biased[:, :, 0:n],
                            biased[:, :, n:n + 1].broadcast_to([P, NT, n]), ALU.is_ge))
                    chain(lambda q, n=n: q.tensor_tensor(
                        beats[:, :, n:NE], biased[:, :, n:NE],
                        biased[:, :, n:n + 1].broadcast_to([P, NT, NE - n]), ALU.is_gt))
                    chain(lambda q, n=n: q.tensor_reduce(rank[:, :, n], beats[:, :, ex], AX.X, ALU.add))
                chain(lambda q: q.tensor_scalar(chosen[:, :, ex], rank[:, :, ex], TOP_K - 0.5, None, ALU.is_lt))
                chain(lambda q: q.tensor_tensor(chosen[:, :, ex], chosen[:, :, ex], prob[:, :, ex], ALU.mult))
                chain(lambda q: q.tensor_reduce(col[:, :, 0], chosen[:, :, ex], AX.X, ALU.add))
                chain(lambda q: q.reciprocal(col[:, :, 1], col[:, :, 0]))
                share_ready[0] = chain(lambda q: q.tensor_tensor(
                    share[:, :, ex], chosen[:, :, ex], spread(col[:, :, 1:2]), ALU.mult))

            gate_here = [None]
            act.wait(pad_made)
            for dst, src in ((gw_raw[:, :, 0:NE], gate_w.rearrange("(c p) e -> p c e", p=P)),
                             (gb[:, 0:NE], gate_b.rearrange("(o e) -> o e", o=1).broadcast_to([P, NE])),
                             (eb[:, 0:NE], biases.rearrange("(o e) -> o e", o=1).broadcast_to([P, NE]))):
                gate_here[0] = gate_in.start(act, dst, src)

            order = [(e, tb, hc) for e in range(NE + 1) for tb in range(NB) for hc in range(HC)]
            NK = (NE + 1) * HC
            loaded = 0
            xnt_ready = {0: layer_norm(0)}
            for _ in range(HC):
                load_weights(loaded)
                loaded += 1
            pending = None
            for e, tb, hc in order:
                if e == 0 and hc == 0 and tb + 1 < NB:
                    xnt_ready[tb + 1] = layer_norm(tb + 1)
                g, g_ready = up(e, tb, hc, xnt_ready[tb])
                if pending:
                    down(*pending)
                pending = (e, tb, hc, g, g_ready)
                if e == 0 and tb == NB - 1 and hc == 1:
                    gate(xnt_ready[NB - 1])
                if loaded < NK and (tb == NB - 1 and hc < HC or tb == 1 and hc == 0 and loaded == (e + 1) * HC):
                    if tb == 1 or (hc >= 1 and loaded < (e + 1) * HC + hc + 1):
                        load_weights(loaded)
                        loaded += 1
            down(*pending)

            with nc.Block() as block:
                block.sync(lambda eng: sp.run(eng))
                block.gpsimd(lambda eng: pool.run(eng))
                block.scalar(lambda eng: act.run(eng))
                block.vector(lambda eng: dve.run(eng))
                block.tensor(lambda eng: pe.run(eng))

        lat_a = store_a[:].rearrange("p (n s t) -> p n s t", n=4, s=2)
        cq, ckvt, ckv_flat, krot = (lat_a[:, n] for n in range(4))
        ckv = ckv_flat.rearrange("p s (t l) -> p s t l", l=LAT)

        with ExitStack() as ctx:
            pe, act, dve, pool = queues(ctx, "lat")
            sp = Queue(None)
            WC = 2 * LAT + DR
            w_raw = tile(ctx, "w_raw", [P, DC, WC])
            w_cat = tile(ctx, "w_cat", [P, 2, DC, WC], F32R)
            cs = tile(ctx, "cs", [P, TB, P])
            sn = tile(ctx, "sn", [P, TB, P])
            c32 = tile(ctx, "c32", [P, 2, 2 * LAT])
            kr_cos = tile(ctx, "kr_cos", [P, 2, DR])
            kr_sin = tile(ctx, "kr_sin", [P, 2, DR])
            kr = tile(ctx, "kr", [P, 2, 2, DR])
            w_in = [Stream(sem(ctx, f"w_in{n}")) for n in range(5)]
            here = [w_in[n].start(sp, w_raw[:, :, a:a + w], src.rearrange("(c p) n -> p c n", p=P))
                    for n, (a, w, src) in enumerate(((0, LAT, wdkvt), (LAT, LAT, wdqt), (2 * LAT, DR, wkrt)))]
            here.append(w_in[3].start(sp, cs[:], rope_cos))
            here.append(w_in[4].start(sp, sn[:], rope_sin))
            act.wait(*here[:3])
            w_hi = act.do(lambda q: q.activation(w_cat[:, 0], w_raw[:], ACT.Copy))
            dve.wait(w_hi, *here)
            w_lo = dve.do(lambda q: q.tensor_tensor(w_cat[:, 1], w_raw[:], w_cat[:, 0].bitcast(F32), ALU.subtract))
            ring = Ring([Slot(b[:]) for b in banks] + [Slot(score_banks[:, i, :]) for i in range(3)])
            c_ring = Ring([Slot(i) for i in range(2)])
            half = DR // 2

            def project(t):
                bank, c = ring.next(), c_ring.next()
                i = c.ap
                cols = slice(t * P, (t + 1) * P)
                pe.wait(w_lo, *bank.free)
                pairs = []
                for d in range(DC):
                    pairs += split3(xnt_hi[:, d, cols], xnt_lo[:, d, cols], w_cat[:, 0, d, :], w_cat[:, 1, d, :])
                done = product(pe, bank.ap[:, 0:WC], pairs)
                act.wait(done, *c.free)
                act.do(lambda q: q.activation(c32[:, i, :], bank.ap[:, 0:2 * LAT], ACT.Copy))
                hi = act.do(lambda q: q.activation(ckv[:, 0, t, :], bank.ap[:, 0:LAT], ACT.Copy))
                dve.wait(hi, *c.free)
                dve.do(lambda q: q.tensor_tensor(ckv[:, 1, t, :], bank.ap[:, 0:LAT],
                                                 ckv[:, 0, t, :].bitcast(F32), ALU.subtract))
                k1, k2 = (bank.ap[:, 2 * LAT + n * half:2 * LAT + (n + 1) * half] for n in range(2))
                j = t % TB
                dve.do(lambda q: q.tensor_tensor(kr_cos[:, i, :], bank.ap[:, 2 * LAT:WC], cs[:, j, 0:DR], ALU.mult))
                dve.do(lambda q: q.tensor_tensor(kr_sin[:, i, 0:half], k2, sn[:, j, 0:half], ALU.mult))
                read = dve.do(lambda q: q.tensor_tensor(kr_sin[:, i, half:DR], k1, sn[:, j, half:DR], ALU.mult))
                bank.free = [read]
                dve.wait(read)
                for n in range(2):
                    ready = dve.do(lambda q, n=n: q.tensor_tensor(kr[:, i, n, :], kr_cos[:, i, :], kr_sin[:, i, :],
                                                                  ALU.add))
                return t, c, [hi, ready]

            def turn(t, c, ready):
                bank, i = ring.next(), c.ap
                cols = slice(t * P, (t + 1) * P)
                pe.wait(*ready, *bank.free)
                pe.quiet(lambda q: q.transpose(bank.ap[:, 0:P], c32[:, i, 0:LAT], ident[:]))
                pe.quiet(lambda q: q.transpose(bank.ap[:, P:2 * P], c32[:, i, LAT:2 * LAT], ident[:]))
                done = pe.do(lambda q: q.transpose(bank.ap[:, 2 * P:3 * P],
                                                   kr[:, i].rearrange("p n d -> p (n d)"), ident[:]))
                c.free = [done]
                act.wait(done)
                for n, dst in enumerate((ckvt, cq, krot)):
                    hi = act.do(lambda q, n=n, dst=dst: q.activation(
                        dst[:, 0, cols], bank.ap[:, n * P:(n + 1) * P], ACT.Copy))
                dve.wait(hi)
                for n, dst in enumerate((ckvt, cq, krot)):
                    lo = dve.do(lambda q, n=n, dst=dst: q.tensor_tensor(
                        dst[:, 1, cols], bank.ap[:, n * P:(n + 1) * P], dst[:, 0, cols].bitcast(F32), ALU.subtract))
                bank.free = [lo]

            held = None
            for t in range(NT):
                now = project(t)
                if held:
                    turn(*held)
                held = now
            turn(*held)
            with nc.Block() as block:
                block.sync(lambda eng: sp.run(eng))
                block.scalar(lambda eng: act.run(eng))
                block.vector(lambda eng: dve.run(eng))
                block.tensor(lambda eng: pe.run(eng))

        with ExitStack() as ctx:
            pe, act, dve, pool = queues(ctx, "att")
            sp = Queue(None)
            KT = SEQ // P
            WIDTH = [SEQ - k * P for k in range(KT)]
            AT = [sum(WIDTH[:k]) for k in range(KT)]
            PW = sum(WIDTH)
            SCORE = [(0, 0), (1, 0), (2, 0), (2, WIDTH[2])]

            at = [0]

            def carve(n):
                at[0] += n
                return store_b[:, at[0] - n:at[0]]

            qc_ring = Ring([Slot(carve(1024).rearrange("p (s t) -> p s t", s=2)) for _ in range(2)])
            qr_ring = Ring([Slot(carve(1024).rearrange("p (h t) -> p h t", h=2)) for _ in range(2)])
            ph_ring = Ring([Slot(carve(PW)) for _ in range(2)])
            pl_ring = Ring([Slot(carve(PW)) for _ in range(2)])
            o_ring = Ring([Slot(carve(1024).rearrange("p (s t) -> p s t", s=2)) for _ in range(2)])
            m_slots = [Slot(carve(2 * 2 * P).rearrange("p (h s l) -> p h s l", h=2, s=2)) for _ in range(2)]
            v_slots = [Slot(carve(2 * 2 * D).rearrange("p (h s d) -> p h s d", h=2, s=2)) for _ in range(2)]
            p_store = tile(ctx, "p_store", [P, 2, PW])
            sum_store = tile(ctx, "sum_store", [P, 2, SEQ])
            r_store = tile(ctx, "r_store", [P, 2, TB, P])
            rc_store = tile(ctx, "rc_store", [P, TB, P])
            rs_store = tile(ctx, "rs_store", [P, TB, P])
            raw = tile(ctx, "raw", [P, 2, 3 * P + D])
            cs = tile(ctx, "cs2", [P, TB, P])
            sn = tile(ctx, "sn2", [P, TB, P])
            wqr = tile(ctx, "wqr", [P, 2, HEADS * DR], F32R)
            ones = tile(ctx, "ones", [P, 1])
            inv_store = tile(ctx, "inv_store", [P, 4, TB])
            p_ring = Ring([Slot(p_store[:, i, :]) for i in range(2)])
            sum_ring = Ring([Slot(sum_store[:, i, :]) for i in range(2)])
            r_ring = Ring([Slot(r_store[:, i]) for i in range(2)])
            inv_ring = Ring([Slot(inv_store[:, i, :]) for i in range(4)])
            rope_tmp = Slot(None)

            const_in = [Stream(sem(ctx, f"const_in{n}")) for n in range(3)]
            raw_in = [Stream(sem(ctx, f"raw_in{n}_{i}")) for n in range(2) for i in range(4)]
            out_sem = [Stream(sem(ctx, f"out_sent{b}")) for b in range(NB)]

            ones_made = pool.do(lambda q: q.memset(ones[:], 1.0))
            wqr_raw = p_store[:].rearrange("p a b -> p (a b)")[:, 0:HEADS * DR]
            wqr_here = const_in[0].start(sp, wqr_raw, wqrt)
            cs_here = const_in[1].start(sp, cs[:], rope_cos)
            sn_here = const_in[2].start(sp, sn[:], rope_sin)
            act.wait(wqr_here)
            t = act.do(lambda q: q.activation(wqr[:, 0, :], wqr_raw, ACT.Copy))
            dve.wait(t)
            wqr_ready = dve.do(lambda q: q.tensor_tensor(wqr[:, 1, :], wqr_raw, wqr[:, 0, :].bitcast(F32),
                                                         ALU.subtract))
            for s in p_ring.slots:
                s.free = [wqr_ready]

            q_banks = Ring([Slot(b[:]) for b in banks[0:2]])
            y_banks = Ring([Slot(b[:]) for b in banks[2:4]])
            o_bank = Slot(banks[4][:])
            score = Slot(score_banks[:])
            score_read = [None]
            inv_read = [None]
            raw_free = [[], []]
            W = {}

            def head_weights(p, h):
                n, i = 2 * p + h, h
                rows = slice(n * P, (n + 1) * P)
                sp.wait(*raw_free[i])
                got = [raw_in[4 * i + j].start(sp, raw[:, i, a:a + w], src[rows, :]) for j, (a, w, src) in
                       enumerate(((0, P, wuq), (P, P, wuk), (2 * P, P, wuv), (3 * P, D, wot)))]
                m, v = m_slots[p % 2].ap[:, h], v_slots[p % 2].ap[:, h]
                ready = []
                for dst, a, b, w in ((m, 0, P, P), (v, 2 * P, 3 * P, D)):
                    bank = q_banks.next()
                    pe.wait(*got, *bank.free)
                    done = pe.do(lambda q, a=a, b=b, w=w, bank=bank: q.matmul(
                        bank.ap[:, 0:w], raw[:, i, a:a + P], raw[:, i, b:b + w], start=True, stop=True))
                    act.wait(done)
                    hi = act.do(lambda q, dst=dst, w=w, bank=bank: q.activation(
                        dst[:, 0, :], bank.ap[:, 0:w], ACT.Copy))
                    dve.wait(hi)
                    lo = dve.do(lambda q, dst=dst, w=w, bank=bank: q.tensor_tensor(
                        dst[:, 1, :], bank.ap[:, 0:w], dst[:, 0, :].bitcast(F32), ALU.subtract))
                    bank.free = [lo]
                    ready.append(lo)
                raw_free[i] = [done]
                W[p, h] = (m, v, ready[0], ready[1])

            def rope_rows(p, b):
                bank, r = q_banks.next(), r_ring.next()
                pe.wait(wqr_ready, *bank.free)
                for t in range(TB):
                    cols = slice(b * SEQ + t * P, b * SEQ + (t + 1) * P)
                    w = slice(p * P, (p + 1) * P)
                    done = product(pe, bank.ap[:, t * P:(t + 1) * P],
                                   split3(cq[:, 0, cols], cq[:, 1, cols], wqr[:, 0, w], wqr[:, 1, w]))
                halves = bank.ap.rearrange("p (t h u d) -> p (t h) u d", t=TB, h=2, u=2)
                sn_h = sn[:].rearrange("p t (h u d) -> p (t h) u d", h=2, u=2)
                rs_h = rs_store[:].rearrange("p t (h u d) -> p (t h) u d", h=2, u=2)
                dve.wait(done, cs_here, sn_here, *rope_tmp.free)
                dve.do(lambda q: q.tensor_tensor(rc_store[:], bank.ap.rearrange("p (t n) -> p t n", t=TB), cs[:],
                                                 ALU.mult))
                dve.do(lambda q: q.tensor_tensor(rs_h[:, :, 0, :], halves[:, :, 1, :], sn_h[:, :, 0, :], ALU.mult))
                read = dve.do(lambda q: q.tensor_tensor(rs_h[:, :, 1, :], halves[:, :, 0, :], sn_h[:, :, 1, :],
                                                        ALU.mult))
                bank.free = [read]
                pool.wait(read, *r.free)
                ready = pool.do(lambda q: q.tensor_tensor(r.ap, rc_store[:], rs_store[:], ALU.add))
                rope_tmp.free = [ready]
                return r, ready

            def rope_turn(r, ready):
                bank, qr = q_banks.next(), qr_ring.next()
                pe.wait(ready, *bank.free)
                for t in range(TB):
                    turn = (lambda q, t=t: q.transpose(bank.ap[:, t * P:(t + 1) * P], r.ap[:, t, :], ident[:]))
                    if t < TB - 1:
                        pe.quiet(turn)
                done = pe.do(turn)
                r.free = [done]
                act.wait(done, *qr.free)
                for h in range(2):
                    rows = slice(h * DR, (h + 1) * DR)
                    hi = act.do(lambda q, h=h, rows=rows: q.activation(qr.ap[rows, h, :], bank.ap[rows, :], ACT.Copy))
                dve.wait(hi)
                for h in range(2):
                    rows, other = slice(h * DR, (h + 1) * DR), slice((1 - h) * DR, (2 - h) * DR)
                    lo = dve.do(lambda q, h=h, rows=rows, other=other: q.tensor_tensor(
                        qr.ap[other, h, :], bank.ap[rows, :], qr.ap[rows, h, :].bitcast(F32), ALU.subtract))
                bank.free = [lo]
                return qr, lo

            def queries(u):
                p, b, h = u
                m, _, m_ready, _ = W[p, h]
                bank, qc = q_banks.next(), qc_ring.next()
                toks = slice(b * SEQ, (b + 1) * SEQ)
                pe.wait(m_ready, *bank.free)
                done = product(pe, bank.ap, split3(m[:, 0, :], m[:, 1, :], cq[:, 0, toks], cq[:, 1, toks]))
                act.wait(done, *qc.free)
                hi = act.do(lambda q: q.activation(qc.ap[:, 0, :], bank.ap, ACT.Copy))
                dve.wait(hi)
                lo = dve.do(lambda q: q.tensor_tensor(qc.ap[:, 1, :], bank.ap, qc.ap[:, 0, :].bitcast(F32),
                                                      ALU.subtract))
                bank.free = [lo]
                return qc, lo

            def scores(u, qc, qc_ready, qr, qr_ready):
                p, b, h = u
                pe.wait(qc_ready, qr_ready, score_read[0], inv_read[0])
                near = slice(h * DR, (h + 1) * DR)
                done = []
                for k in range(KT):
                    keys = slice(b * SEQ + k * P, b * SEQ + (k + 1) * P)
                    toks = slice(k * P, SEQ)
                    bank, off = SCORE[k]
                    pairs = split3(ckvt[:, 0, keys], ckvt[:, 1, keys], qc.ap[:, 0, toks], qc.ap[:, 1, toks])
                    pairs += [(krot[:, 0, keys], qr.ap[:, h, toks]), (krot[near, 1, keys], qr.ap[near, h, toks])]
                    done.append(product(pe, score_banks[:, bank, off:off + WIDTH[k]], pairs))
                qc.free = [done[-1]]
                if h == 1:
                    qr.free = [done[-1]]
                w, ph, pl, sm = p_ring.next(), ph_ring.next(), pl_ring.next(), sum_ring.next()
                act.wait(done[0], *w.free)
                act.do(lambda q: q.activation(w.ap[:, 0:WIDTH[0]], score_banks[:, 0, :], ACT.Exp, scale=SCALE))
                act.wait(done[-1])
                exps = act.do(lambda q: q.activation(
                    w.ap[:, WIDTH[0]:PW].rearrange("p (n t) -> p n t", n=2), score_banks[:, 1:3, 0:WIDTH[1]],
                    ACT.Exp, scale=SCALE))
                score_read[0] = exps
                dve.wait(exps)
                clipped = dve.do(lambda q: q.tensor_scalar(
                    w.ap, w.ap, float(np.exp(-CLIP * SCALE)), float(np.exp(CLIP * SCALE)), ALU.max, ALU.min))
                return w, ph, pl, sm, clipped

            def weigh(u, w, ph, pl, sm, clipped):
                pool.wait(clipped)
                for k in range(KT):
                    masked = pool.do(lambda q, k=k: q.affine_select(
                        out=w.ap[:, AT[k]:AT[k] + P], in_=w.ap[:, AT[k]:AT[k] + P], compare_op=ALU.is_ge,
                        fill=0.0, base=0, pattern=[[1, P]], channel_multiplier=-1))
                act.wait(masked, *ph.free)
                hi = act.do(lambda q: q.activation(ph.ap, w.ap, ACT.Copy))
                pool.wait(masked, *sm.free)
                pool.do(lambda q: q.tensor_tensor(sm.ap[:, P:SEQ], w.ap[:, P:SEQ], w.ap[:, AT[1]:AT[2]], ALU.add))
                for k in range(2, KT):
                    pool.wait(Ticket(pool.sem, pool.count))
                    summed = pool.do(lambda q, k=k: q.tensor_tensor(
                        sm.ap[:, k * P:SEQ], sm.ap[:, k * P:SEQ], w.ap[:, AT[k]:AT[k] + WIDTH[k]], ALU.add))
                return w, ph, pl, sm, hi, summed

            def weigh_low(u, w, ph, pl, sm, hi, summed):
                dve.wait(hi, *pl.free)
                lo = dve.do(lambda q: q.tensor_tensor(pl.ap, w.ap, ph.ap.bitcast(F32), ALU.subtract))
                return w, ph, pl, sm, lo, summed

            def attend(u, w, ph, pl, sm, lo, summed):
                p, b, h = u
                pe.wait(lo, *o_bank.free)
                for k in range(KT):
                    t = b * TB + k
                    cols = slice(AT[k], AT[k] + WIDTH[k])
                    done = product(pe, o_bank.ap[:, k * P:SEQ],
                                   split3(ckv[:, 0, t, :], ckv[:, 1, t, :], ph.ap[:, cols], pl.ap[:, cols]),
                                   first=k == 0, last=k == KT - 1)
                ph.free = pl.free = [done]
                pe.wait(summed, ones_made, score_read[0])
                den = score_banks[:, 1, WIDTH[1]:WIDTH[1] + TB]
                for t in range(TB):
                    src = w.ap[:, 0:P] if t == 0 else sm.ap[:, t * P:(t + 1) * P]
                    dens = pe.do(lambda q, t=t, src=src: q.matmul(den[:, t:t + 1], src, ones[:],
                                                                  start=True, stop=True))
                sm.free = [dens]
                w.free = [dens]
                inv, o = inv_ring.next(), o_ring.next()
                dve.wait(dens, *inv.free)
                inverted = dve.do(lambda q: q.reciprocal(inv.ap, den))
                inv_read[0] = inverted
                act.wait(done, *o.free)
                hi = act.do(lambda q: q.activation(o.ap[:, 0, :], o_bank.ap, ACT.Copy))
                dve.wait(hi)
                o_lo = dve.do(lambda q: q.tensor_tensor(o.ap[:, 1, :], o_bank.ap, o.ap[:, 0, :].bitcast(F32),
                                                        ALU.subtract))
                o_bank.free = [o_lo]
                return o, o_lo, inv, inverted

            acc_done = {}

            def output(u, o, o_ready, inv, inverted):
                p, b, h = u
                _, v, _, v_ready = W[p, h]
                pe.wait(o_ready, v_ready)
                for tt in range(TB):
                    y = y_banks.next()
                    cols = slice(tt * P, (tt + 1) * P)
                    pe.wait(*y.free)
                    done = product(pe, y.ap, split3(o.ap[:, 0, cols], o.ap[:, 1, cols], v[:, 0, :], v[:, 1, :]))
                    t = b * TB + tt
                    dve.wait(done, inverted, acc_done.get(t))
                    y_read = dve.do(lambda q, y=y, t=t, tt=tt: q.scalar_tensor_tensor(
                        acc[:, t, :], y.ap, inv.ap[:, tt:tt + 1], acc[:, t, :], ALU.mult, ALU.add))
                    y.free = [y_read]
                    acc_done[t] = y_read
                o.free = [done]
                inv.free = [y_read]
                if (p, h) == (PAIRS - 1, 1):
                    sp.wait(y_read)
                    sent.append(out_sem[b].start(sp, out_t[:, b * TB:(b + 1) * TB, :],
                                                 acc[:, b * TB:(b + 1) * TB, :]))

            sent = []
            units = [(p, b, h) for p in range(PAIRS) for b in range(NB) for h in range(2)]
            head_weights(0, 0)
            head_weights(0, 1)
            rotated = rope_rows(0, 0)
            qr = rope_turn(*rotated)
            qc = queries(units[0])
            weighed = attended = None
            for i in range(len(units) + 2):
                u = units[i] if i < len(units) else None
                after = units[i + 1] if i + 1 < len(units) else None
                if u:
                    now = (u, *scores(u, *qc, *qr))
                    p, b, h = u
                    if h == 1 and after:
                        qr = rope_turn(*rotated)
                    if after:
                        qc = queries(after)
                    if h == 0 and i + 2 < len(units):
                        rotated = rope_rows(*units[i + 2][:2])
                    if b == 2 and p + 1 < PAIRS:
                        head_weights(p + 1, h)
                nxt = None
                if weighed:
                    nxt = (weighed[0], *attend(*weighed))
                if u:
                    now = (u, *weigh(*now))
                if attended:
                    output(*attended)
                if u:
                    now = (u, *weigh_low(*now))
                attended = nxt
                weighed = now if u else None
            sp.wait(*sent)
            with nc.Block() as block:
                block.sync(lambda eng: sp.run(eng))
                block.gpsimd(lambda eng: pool.run(eng))
                block.scalar(lambda eng: act.run(eng))
                block.vector(lambda eng: dve.run(eng))
                block.tensor(lambda eng: pe.run(eng))


def rope_tables(seq, width, tile):
    inv_freq = (np.float32(10000.0) ** (-np.arange(0, width, 2, dtype=np.float32) / np.float32(width)))
    ang = np.arange(seq, dtype=np.float32)[:, None] * inv_freq.astype(np.float32)[None, :]
    c, s = np.cos(ang).astype(np.float32), np.sin(ang).astype(np.float32)
    cos = np.concatenate([c, c, c, c], axis=1).reshape(seq // tile, tile, 2 * width)
    sin = np.concatenate([-s, s, -s, s], axis=1).reshape(seq // tile, tile, 2 * width)
    return np.ascontiguousarray(cos.transpose(1, 0, 2)), np.ascontiguousarray(sin.transpose(1, 0, 2))


def kernel(**inputs):
    import concourse.bacc as bacc
    from concourse.bass_utils import run_bass_kernel_spmd

    att, ffn = "L0_attn_", "L0_ffn_"
    a = {n: np.asarray(v) for n, v in inputs.items()}
    d_rot = a[att + "W_KR"].shape[0]
    heads = a[att + "W_QR"].shape[0] // d_rot
    wqr = a[att + "W_QR"].reshape(heads, d_rot // 2, 2, -1).transpose(0, 2, 1, 3).reshape(heads * d_rot, -1)
    wkr = a[att + "W_KR"].reshape(d_rot // 2, 2, -1).transpose(1, 0, 2).reshape(d_rot, -1)
    cos, sin = rope_tables(a[att + "x"].shape[1], d_rot, 128)
    laid = {
        "x": a[att + "x"], "wdqt": a[att + "W_DQ"].T, "wuq": a[att + "W_UQ"], "wqrt": wqr.T,
        "wdkvt": a[att + "W_DKV"].T, "wuk": a[att + "W_UK"], "wuv": a[att + "W_UV"], "wkrt": wkr.T,
        "wot": a[att + "W_O"].T,
        "w1": a[ffn + "W1"], "wg": a[ffn + "Wg"], "w2": a[ffn + "W2"],
        "ws1": a[ffn + "Ws1"], "wsg": a[ffn + "Wsg"], "ws2": a[ffn + "Ws2"],
        "gate_w": a[ffn + "gate_w"], "gate_b": a[ffn + "gate_b"], "biases": a[ffn + "biases"],
        "rope_cos": cos, "rope_sin": sin,
    }
    nc = bacc.Bacc("TRN2", target_bir_lowering=False, num_devices=1)
    arrays, args = {}, []
    for name, v in laid.items():
        arrays[f"in_{name}"] = np.ascontiguousarray(v)
        args.append(nc.dram_tensor(f"in_{name}", v.shape, F32, kind="ExternalInput").ap())
    args.append(nc.dram_tensor("out_0", a[att + "x"].shape, F32, kind="ExternalOutput").ap())
    program(nc, *args)
    r = run_bass_kernel_spmd(nc, [arrays], core_ids=[0])
    return r.results[0]["out_0"]
```

```python
from contextlib import ExitStack

import numpy as np

import concourse.bass as bass
from concourse import mybir

ALU = mybir.AluOpType
ACT = mybir.ActivationFunctionType
AX = mybir.AxisListType
F32 = mybir.dt.float32
F32R = mybir.dt.float32r

P = 128
BANK = 512
LN_EPS = 1e-5
TOP_K = 3
CLIP = 80.0


class Ticket:

    def __init__(self, sem, value):
        self.sem, self.value = sem, value


class Queue:

    def __init__(self, sem):
        self.sem, self.steps, self.count, self.waited = sem, [], 0, {}

    def wait(self, *tickets):
        for t in tickets:
            if t is None or self.waited.get(id(t.sem), 0) >= t.value:
                continue
            self.waited[id(t.sem)] = t.value
            self.steps.append(lambda eng, t=t: eng.wait_ge(t.sem, t.value))

    def do(self, make):
        self.count += 1
        self.steps.append(lambda eng: make(eng).then_inc(self.sem, 1))
        return Ticket(self.sem, self.count)

    def quiet(self, make):
        self.steps.append(lambda eng: make(eng))

    def run(self, eng):
        for step in self.steps:
            step(eng)


class Stream:

    def __init__(self, sem):
        self.sem, self.count = sem, 0

    def start(self, queue, out, in_):
        self.count += 16
        queue.steps.append(lambda eng: eng.dma_start(out, in_).then_inc(self.sem, 16))
        return Ticket(self.sem, self.count)


class Slot:

    def __init__(self, ap):
        self.ap, self.free, self.ready = ap, [], []


class Ring:
    def __init__(self, slots):
        self.slots, self.at = slots, 0

    def next(self):
        s = self.slots[self.at % len(self.slots)]
        self.at += 1
        return s


def product(pe, out, pairs, first=True, last=True):
    t = None
    for n, (a, b) in enumerate(pairs):
        start, stop = first and n == 0, last and n == len(pairs) - 1
        make = lambda eng, a=a, b=b, start=start, stop=stop: eng.matmul(out, a, b, start=start, stop=stop)
        if n == len(pairs) - 1:
            t = pe.do(make)
        else:
            pe.quiet(make)
    return t


def split3(a_hi, a_lo, b_hi, b_lo):
    return [(a_hi, b_hi), (a_hi, b_lo), (a_lo, b_hi)]


def program(nc, x, wdqt, wuq, wqrt, wqrt_swapped, wdkvt, wuk, wuv, wkrt, wot, w1, wg, w2, ws1, wsg, ws2,
            gate_w, gate_b, biases, rope_cos, rope_sin, rope_cos_t, rope_sin_t, out):
    BATCH, SEQ, D = x.shape
    TOK = BATCH * SEQ
    NT = TOK // P
    NB = TOK // BANK
    TB = BANK // P
    NE, _, HID = w1.shape
    DC, HC = D // P, HID // P
    LAT = wdqt.shape[1]
    DR = wkrt.shape[1]
    HEADS = wuq.shape[0] // P
    PAIRS = HEADS // 2
    DH = wuq.shape[0] // HEADS
    SCALE = float(1.0 / np.sqrt(np.float32(DH + DR)))
    assert SEQ == BANK and LAT == P and 2 * DR == P and DH == P and D == BANK

    x_t = x.rearrange("b (t p) d -> p (b t) d", p=P)
    out_t = out.rearrange("b (t p) d -> p (b t) d", p=P)

    with ExitStack() as whole:
        def tile(ctx, name, shape, dt=F32):
            return ctx.enter_context(nc.sbuf_tensor(name, shape, dt))

        def sem(ctx, name):
            return ctx.enter_context(nc.semaphore(name))

        pe, act, dve, pool = (Queue(sem(whole, f"{n}_done")) for n in ("pe", "act", "dve", "pool"))
        sp = Queue(None)

        def all_done():
            return [Ticket(q.sem, q.count) for q in (pe, act, dve, pool)]

        bank_slots = [Slot(whole.enter_context(nc.psum_tensor(f"bank{i}", [P, BANK], F32))[:]) for i in range(8)]

        acc = tile(whole, "acc", [P, NT, D])
        store_a = tile(whole, "store_a", [P, 16384], F32R)
        store_b = tile(whole, "store_b", [P, 16384], F32R)
        ident = tile(whole, "ident", [P, P])
        WC = 2 * LAT + DR
        w_cat = tile(whole, "w_cat", [P, 2, DC, WC], F32R)
        acc_done = {}

        xnt = store_b[:].rearrange("p (s c t) -> p s c t", s=2, c=DC)
        xnt_hi, xnt_lo = xnt[:, 0], xnt[:, 1]

        with ExitStack() as ctx:
            UPS, DNS = 5, 6
            up_w = store_a[:, 0:UPS * 2048].rearrange("p (n s m c h) -> p n s m c h", n=UPS, s=2, m=2, c=DC)
            dn_w = store_a[:, UPS * 2048:UPS * 2048 + DNS * 1024].rearrange("p (n s d) -> p n s d", n=DNS, s=2)
            up_slots = [Slot(up_w[:, n]) for n in range(UPS)]
            dn_slots = [Slot(dn_w[:, n]) for n in range(DNS)]
            raw_up = tile(ctx, "raw_up", [P, 2, 2, DC, P])
            raw_dn = tile(ctx, "raw_dn", [P, 2, D])
            g_store = tile(ctx, "g_store", [P, 2, 2, BANK], F32R)
            s_store = tile(ctx, "s_store", [P, 2, BANK])
            h_store = tile(ctx, "h_store", [P, 2, BANK])
            stats = tile(ctx, "stats", [P, NT, 6])
            mv = tile(ctx, "mv", [P, NT, 2])
            var_eps = tile(ctx, "var_eps", [P, NT])
            rstd = tile(ctx, "rstd", [P, NT])
            neg_half = tile(ctx, "neg_half", [P, NT])
            gw_raw = tile(ctx, "gw_raw", [P, DC, 8])
            gw = tile(ctx, "gw", [P, DC, 16], F32R)
            gb = tile(ctx, "gb", [P, 8])
            eb = tile(ctx, "eb", [P, 8])
            logit = tile(ctx, "logit", [P, NT, 8])
            prob = tile(ctx, "prob", [P, NT, 8])
            biased = tile(ctx, "biased", [P, NT, 8])
            beats = tile(ctx, "beats", [P, NT, 8])
            rank = tile(ctx, "rank", [P, NT, 8])
            chosen = tile(ctx, "chosen", [P, NT, 8])
            share = tile(ctx, "share", [P, NT, 8])
            col = tile(ctx, "col", [P, NT, 2])

            x_in = [Stream(sem(ctx, f"x_in{t}")) for t in range(NT)]
            gate_in = Stream(sem(ctx, "gate_in"))
            wu_in = [Stream(sem(ctx, f"wu_in{n}")) for n in range(2)]
            wg_in = [Stream(sem(ctx, f"wg_in{n}")) for n in range(2)]
            wd_in = [Stream(sem(ctx, f"wd_in{n}")) for n in range(2)]
            cat_in = [Stream(sem(ctx, f"cat_in{n}")) for n in range(3)]

            x_here = {}

            def load_x(b):
                for t in range(b * TB, (b + 1) * TB):
                    x_here[t] = x_in[t].start(sp, acc[:, t, :], x_t[:, t, :])

            t = pool.do(lambda e: e.memset(ident[:], 0.0))
            pool.wait(t)
            ident_made = pool.do(lambda e: e.affine_select(
                out=ident[:], in_=ident[:], compare_op=ALU.not_equal, fill=1.0, base=0,
                pattern=[[-1, P]], channel_multiplier=1))
            half_made = pool.do(lambda e: e.memset(neg_half[:], -0.5))
            pad_made = pool.do(lambda e: e.memset(gw_raw[:], 0.0))

            up_ring = Ring(bank_slots[0:4])
            y_slots = bank_slots[4:8]
            s_ring = Ring([Slot(s_store[:, i, :]) for i in range(2)])

            def statistics(b):
                tiles = range(b * TB, (b + 1) * TB)
                for t in tiles:
                    dve.wait(x_here[t])
                    got = dve.do(lambda e, t=t: e.bn_stats(out=stats[:, t, :], in_=acc[:, t, :]))
                dve.wait(got)
                for t in tiles:
                    got = dve.do(lambda e, t=t: e.bn_aggr(out=mv[:, t, :], in_=stats[:, t, :]))
                dve.wait(got)
                var_ready = dve.do(lambda e: e.tensor_scalar(
                    var_eps[:, b * TB:(b + 1) * TB], mv[:, b * TB:(b + 1) * TB, 1], LN_EPS, None, ALU.add))
                pool.wait(var_ready, half_made)
                rstd_ready[b] = pool.do(lambda e: e.tensor_tensor(
                    rstd[:, b * TB:(b + 1) * TB], var_eps[:, b * TB:(b + 1) * TB],
                    neg_half[:, b * TB:(b + 1) * TB], ALU.pow))

            rstd_ready, xnt_ready = {}, {}

            def normalise(t):
                xn = s_ring.next()
                dve.wait(rstd_ready[t // TB], *xn.free)
                xn_ready = dve.do(lambda e: e.tensor_scalar(
                    xn.ap, acc[:, t, :], mv[:, t, 0:1], rstd[:, t:t + 1], ALU.subtract, ALU.mult))
                return t, xn, xn_ready

            def turn_rows(t, xn, xn_ready):
                bank = up_ring.next()
                pe.wait(xn_ready, ident_made, *bank.free)
                for c in range(DC):
                    turned = pe.do(lambda e, c=c: e.transpose(
                        bank.ap[:, c * P:(c + 1) * P], xn.ap[:, c * P:(c + 1) * P], ident[:]))
                xn.free = [turned]
                src = bank.ap.rearrange("p (c t) -> p c t", c=DC)
                cols = slice(t * P, (t + 1) * P)
                act.wait(turned)
                hi = act.do(lambda e: e.activation(xnt_hi[:, :, cols], src, ACT.Copy))
                dve.wait(hi)
                lo = dve.do(lambda e: e.tensor_tensor(
                    xnt_lo[:, :, cols], src, xnt_hi[:, :, cols].bitcast(F32), ALU.subtract))
                bank.free = [lo]
                xnt_ready[t // TB] = lo

            def load_weights(k):
                e, hc = divmod(k, HC)
                r = k % 2
                src1, srcg, src2 = (ws1, wsg, ws2) if e == 0 else (w1[e - 1], wg[e - 1], w2[e - 1])
                cols = slice(hc * P, (hc + 1) * P)
                sp.wait(*raw_free[r])
                a = wu_in[r].start(sp, raw_up[:, r, 0], src1.rearrange("(c p) h -> p c h", p=P)[:, :, cols])
                b = wg_in[r].start(sp, raw_up[:, r, 1], srcg.rearrange("(c p) h -> p c h", p=P)[:, :, cols])
                c = wd_in[r].start(sp, raw_dn[:, r], src2[cols, :])
                up, dn = up_slots[k % UPS], dn_slots[k % DNS]
                act.wait(a, b, *up.free)
                up_hi = act.do(lambda g: g.activation(up.ap[:, 0], raw_up[:, r], ACT.Copy))
                act.wait(c, *dn.free)
                dn_hi = act.do(lambda g: g.activation(dn.ap[:, 0], raw_dn[:, r], ACT.Copy))
                rest = dve if k == 0 else pool
                rest.wait(up_hi)
                up_lo = rest.do(lambda g: g.tensor_tensor(
                    up.ap[:, 1], raw_up[:, r], up.ap[:, 0].bitcast(F32), ALU.subtract))
                rest.wait(dn_hi)
                dn_lo = rest.do(lambda g: g.tensor_tensor(
                    dn.ap[:, 1], raw_dn[:, r], dn.ap[:, 0].bitcast(F32), ALU.subtract))
                raw_free[r] = [dn_lo]
                weights[k] = (up.ap, dn.ap, up_lo, dn_lo)

            raw_free = {0: [], 1: []}
            weights = {}
            g_ring = Ring([Slot(g_store[:, i]) for i in range(2)])
            h_ring = Ring([Slot(h_store[:, i, :]) for i in range(2)])

            def up(e, tb, hc):
                k = e * HC + hc
                w, _, w_ready, _ = weights[k]
                toks = slice(tb * BANK, (tb + 1) * BANK)
                bank1, bankg = up_ring.next(), up_ring.next()
                done = []
                for m, bank in ((0, bank1), (1, bankg)):
                    pe.wait(w_ready, xnt_ready[tb], *bank.free)
                    pairs = []
                    for c in range(DC):
                        pairs += split3(w[:, 0, m, c, :], w[:, 1, m, c, :],
                                        xnt_hi[:, c, toks], xnt_lo[:, c, toks])
                    done.append(product(pe, bank.ap, pairs))
                if tb == NB - 1:
                    up_slots[k % UPS].free = [done[1]]
                s, h, g = s_ring.next(), h_ring.next(), g_ring.next()
                act.wait(done[0], *s.free)
                s_ready = act.do(lambda q: q.activation(s.ap, bank1.ap, ACT.Silu))
                bank1.free = [s_ready]
                dve.wait(s_ready, done[1], *h.free)
                h_ready = dve.do(lambda q: q.tensor_tensor(h.ap, bankg.ap, s.ap, ALU.mult))
                bankg.free = [h_ready]
                s.free = [h_ready]
                act.wait(h_ready, *g.free)
                hi = act.do(lambda q: q.activation(g.ap[:, 0], h.ap, ACT.Copy))
                dve.wait(hi)
                lo = dve.do(lambda q: q.tensor_tensor(g.ap[:, 1], h.ap, g.ap[:, 0].bitcast(F32), ALU.subtract))
                h.free = [lo]
                return g, lo

            def down(e, tb, hc, g, g_ready):
                k = e * HC + hc
                _, w, _, w_ready = weights[k]
                pe.wait(g_ready, w_ready)
                for tt in range(TB):
                    y = y_slots[tt]
                    if hc == 0:
                        pe.wait(*y.free)
                    cols = slice(tt * P, (tt + 1) * P)
                    done = product(pe, y.ap, split3(g.ap[:, 0, cols], g.ap[:, 1, cols], w[:, 0], w[:, 1]),
                                   first=hc == 0, last=hc == HC - 1)
                    if hc == HC - 1:
                        t = tb * TB + tt
                        dve.wait(done, acc_done.get(t))
                        if e == 0:
                            y_read = dve.do(lambda q, y=y, t=t: q.tensor_tensor(
                                acc[:, t, :], y.ap, acc[:, t, :], ALU.add))
                        else:
                            dve.wait(*share_ready)
                            y_read = dve.do(lambda q, y=y, t=t: q.scalar_tensor_tensor(
                                acc[:, t, :], y.ap, share[:, t, e - 1:e], acc[:, t, :], ALU.mult, ALU.add))
                        y.free = [y_read]
                        acc_done[t] = y_read
                g.free = [done]
                if tb == NB - 1:
                    dn_slots[k % DNS].free = [done]

            share_ready, gate_steps = [], []

            def gate():
                act.wait(gate_here[0])
                gw_hi = act.do(lambda q: q.activation(gw[:, :, 0:8], gw_raw[:], ACT.Copy))
                dve.wait(gw_hi)
                gw_lo = dve.do(lambda q: q.tensor_tensor(gw[:, :, 8:16], gw_raw[:], gw[:, :, 0:8].bitcast(F32),
                                                         ALU.subtract))
                back = up_ring.next()
                pe.wait(gw_lo, xnt_ready[NB - 1])
                for b in range(NB):
                    bank, rows = up_ring.next(), h_ring.next()
                    if bank is back:
                        bank = up_ring.next()
                    toks = slice(b * BANK, (b + 1) * BANK)
                    pe.wait(*bank.free)
                    product(pe, bank.ap[0:16, :], [(gw[:, c, :], xnt_hi[:, c, toks]) for c in range(DC)], last=False)
                    done = product(pe, bank.ap[0:8, :], [(gw[:, c, 0:8], xnt_lo[:, c, toks]) for c in range(DC)],
                                   first=False)
                    act.wait(done, *rows.free)
                    copied = act.do(lambda q, rows=rows, bank=bank: q.activation(
                        rows.ap[0:16, :], bank.ap[0:16, :], ACT.Copy))
                    bank.free = [copied]
                    pe.wait(copied, *back.free)
                    for t in range(TB):
                        turned = pe.do(lambda q, b=b, t=t, rows=rows: q.transpose(
                            back.ap[:, (b * TB + t) * 16:(b * TB + t + 1) * 16],
                            rows.ap[0:16, t * P:(t + 1) * P], ident[0:16, 0:16]))
                    rows.free = [turned]
                act.wait(turned)
                both = back.ap[:, 0:NT * 16].rearrange("p (t e) -> p t e", e=16)
                got = act.do(lambda q: q.activation(logit[:], both[:, :, 0:8], ACT.Copy))
                dve.wait(got)
                got = dve.do(lambda q: q.tensor_tensor(logit[:], both[:, :, 8:16], logit[:], ALU.add))
                back.free = [got]
                last = [got]

                def chain(make, queue=dve):
                    def step():
                        queue.wait(last[0])
                        last[0] = queue.do(make)
                    gate_steps.append(step)

                ex = slice(0, NE)

                def over(v):
                    return v.unsqueeze(1).broadcast_to([P, NT, NE])

                def spread(v):
                    return v.broadcast_to([P, NT, NE])

                chain(lambda q: q.tensor_tensor(logit[:, :, ex], logit[:, :, ex], over(gb[:, ex]), ALU.add))
                chain(lambda q: q.tensor_reduce(col[:, :, 0], logit[:, :, ex], AX.X, ALU.max))
                chain(lambda q: q.tensor_tensor(logit[:, :, ex], logit[:, :, ex], spread(col[:, :, 0:1]),
                                                ALU.subtract))
                chain(lambda q: q.activation(prob[:, :, ex], logit[:, :, ex], ACT.Exp), act)
                chain(lambda q: q.tensor_reduce(col[:, :, 0], prob[:, :, ex], AX.X, ALU.add))
                chain(lambda q: q.reciprocal(col[:, :, 1], col[:, :, 0]))
                chain(lambda q: q.tensor_tensor(prob[:, :, ex], prob[:, :, ex], spread(col[:, :, 1:2]), ALU.mult))
                chain(lambda q: q.tensor_tensor(biased[:, :, ex], prob[:, :, ex], over(eb[:, ex]), ALU.add))
                for n in range(NE):
                    if n:
                        chain(lambda q, n=n: q.tensor_tensor(
                            beats[:, :, 0:n], biased[:, :, 0:n],
                            biased[:, :, n:n + 1].broadcast_to([P, NT, n]), ALU.is_ge))
                    chain(lambda q, n=n: q.tensor_tensor(
                        beats[:, :, n:NE], biased[:, :, n:NE],
                        biased[:, :, n:n + 1].broadcast_to([P, NT, NE - n]), ALU.is_gt))
                    chain(lambda q, n=n: q.tensor_reduce(rank[:, :, n], beats[:, :, ex], AX.X, ALU.add))
                chain(lambda q: q.tensor_scalar(chosen[:, :, ex], rank[:, :, ex], TOP_K - 0.5, None, ALU.is_lt))
                chain(lambda q: q.tensor_tensor(chosen[:, :, ex], chosen[:, :, ex], prob[:, :, ex], ALU.mult))
                chain(lambda q: q.tensor_reduce(col[:, :, 0], chosen[:, :, ex], AX.X, ALU.add))
                chain(lambda q: q.reciprocal(col[:, :, 1], col[:, :, 0]))
                chain(lambda q: q.tensor_tensor(share[:, :, ex], chosen[:, :, ex], spread(col[:, :, 1:2]), ALU.mult))
                gate_steps.append(lambda: share_ready.append(last[0]))

            gate_here = [None]
            act.wait(pad_made)
            for dst, src in ((gw_raw[:, :, 0:NE], gate_w.rearrange("(c p) e -> p c e", p=P)),
                             (gb[:, 0:NE], gate_b.rearrange("(o e) -> o e", o=1).broadcast_to([P, NE])),
                             (eb[:, 0:NE], biases.rearrange("(o e) -> o e", o=1).broadcast_to([P, NE]))):
                gate_here[0] = gate_in.start(act, dst, src)

            order = [(e, tb, hc) for e in range(NE + 1) for tb in range(NB) for hc in range(HC)]
            NK = (NE + 1) * HC
            GATE_STEPS_A_CHUNK = 8
            AHEAD = TB + 1
            load_x(0)
            statistics(0)
            load_weights(0)
            load_x(1)
            rows = normalise(0)
            for t in range(1, AHEAD):
                if t == TB:
                    statistics(1)
                following = normalise(t)
                turn_rows(*rows)
                rows = following
            turn_rows(*rows)
            load_weights(1)
            load_weights(2)
            load_x(2)
            load_weights(3)
            load_x(3)
            loaded = HC
            pending = None
            for e, tb, hc in order:
                t = tb * HC + hc + AHEAD
                rows = None
                if e == 0 and t < NT:
                    rows = normalise(t)
                    if (t + 2) % TB == 0 and t + 2 < NT:
                        statistics((t + 2) // TB)
                g, g_ready = up(e, tb, hc)
                if rows:
                    turn_rows(*rows)
                if pending:
                    down(*pending)
                pending = (e, tb, hc, g, g_ready)
                if e == 0 and tb == NB - 1 and hc == 0:
                    gate()
                for step in gate_steps[:GATE_STEPS_A_CHUNK]:
                    step()
                del gate_steps[:GATE_STEPS_A_CHUNK]
                if loaded < NK and (tb == 1 and hc == 0 or tb == NB - 1 and hc >= 1):
                    load_weights(loaded)
                    loaded += 1
                if (e, tb, hc) == (NE, 1, 0):
                    w_raw = raw_up[:].rearrange("p a b c h -> p (a b c h)")[:, 0:DC * WC].rearrange(
                        "p (c n) -> p c n", c=DC)
                    sp.wait(*raw_free[0], *raw_free[1])
                    here = [cat_in[n].start(sp, w_raw[:, :, a:a + w], src.rearrange("(c p) n -> p c n", p=P))
                            for n, (a, w, src) in enumerate(((0, LAT, wdkvt), (LAT, LAT, wdqt), (2 * LAT, DR, wkrt)))]
                    act.wait(*here)
                    cat_hi = act.do(lambda q: q.activation(w_cat[:, 0], w_raw, ACT.Copy))
                    pool.wait(cat_hi)
                    cat_ready = pool.do(lambda q: q.tensor_tensor(w_cat[:, 1], w_raw, w_cat[:, 0].bitcast(F32),
                                                                  ALU.subtract))
            assert not gate_steps and loaded == NK
            down(*pending)

        lat_a = store_a[:].rearrange("p (n s t) -> p n s t", n=4, s=2)
        cq, ckvt, ckv_flat, krot = (lat_a[:, n] for n in range(4))
        ckv = ckv_flat.rearrange("p s (t l) -> p s t l", l=LAT)

        experts_done = all_done()
        with ExitStack() as ctx:
            NG = 5
            p_store = tile(ctx, "p_store", [P, NG + 1, BANK])
            p_flat = p_store[:].rearrange("p n t -> p (n t)")
            at = [0]

            def carve_small(shape):
                n = int(np.prod(shape))
                at[0] += n
                part = p_flat[:, at[0] - n:at[0]]
                names = "abc"[:len(shape)]
                return part.rearrange(f"p ({' '.join(names)}) -> p {' '.join(names)}", **dict(zip(names, shape)))

            cs, sn = carve_small((TB, P)), carve_small((TB, P))
            c32 = carve_small((2, 2 * LAT))
            kr_cos, kr_sin = carve_small((2, DR)), carve_small((2, DR))
            kr = carve_small((2, 2, DR))
            table_in = [Stream(sem(ctx, f"table_in{n}")) for n in range(2)]
            sp.wait(*experts_done)
            tables_here = [table_in[0].start(sp, cs, rope_cos), table_in[1].start(sp, sn, rope_sin)]
            for queue in (act, dve, pool):
                queue.wait(*experts_done)
            dve.wait(*tables_here)
            ring = Ring(bank_slots)
            c_ring = Ring([Slot(i) for i in range(2)])
            half = DR // 2

            def project(t):
                bank, c = ring.next(), c_ring.next()
                i = c.ap
                cols = slice(t * P, (t + 1) * P)
                pe.wait(cat_ready, *bank.free)
                pairs = []
                for d in range(DC):
                    pairs += split3(xnt_hi[:, d, cols], xnt_lo[:, d, cols], w_cat[:, 0, d, :], w_cat[:, 1, d, :])
                done = product(pe, bank.ap[:, 0:WC], pairs)
                act.wait(done, *c.free)
                act.do(lambda q: q.activation(c32[:, i, :], bank.ap[:, 0:2 * LAT], ACT.Copy))
                hi = act.do(lambda q: q.activation(ckv[:, 0, t, :], bank.ap[:, 0:LAT], ACT.Copy))
                dve.wait(hi, *c.free)
                dve.do(lambda q: q.tensor_tensor(ckv[:, 1, t, :], bank.ap[:, 0:LAT],
                                                 ckv[:, 0, t, :].bitcast(F32), ALU.subtract))
                k1, k2 = (bank.ap[:, 2 * LAT + n * half:2 * LAT + (n + 1) * half] for n in range(2))
                j = t % TB
                dve.do(lambda q: q.tensor_tensor(kr_cos[:, i, :], bank.ap[:, 2 * LAT:WC], cs[:, j, 0:DR], ALU.mult))
                dve.do(lambda q: q.tensor_tensor(kr_sin[:, i, 0:half], k2, sn[:, j, 0:half], ALU.mult))
                read = dve.do(lambda q: q.tensor_tensor(kr_sin[:, i, half:DR], k1, sn[:, j, half:DR], ALU.mult))
                bank.free = [read]
                dve.wait(read)
                for n in range(2):
                    ready = dve.do(lambda q, n=n: q.tensor_tensor(kr[:, i, n, :], kr_cos[:, i, :], kr_sin[:, i, :],
                                                                  ALU.add))
                return t, c, [hi, ready], done.value

            def turn(t, c, ready, _):
                bank, i = ring.next(), c.ap
                cols = slice(t * P, (t + 1) * P)
                pe.wait(*ready, *bank.free)
                pe.quiet(lambda q: q.transpose(bank.ap[:, 0:P], c32[:, i, 0:LAT], ident[:]))
                pe.quiet(lambda q: q.transpose(bank.ap[:, P:2 * P], c32[:, i, LAT:2 * LAT], ident[:]))
                done = pe.do(lambda q: q.transpose(bank.ap[:, 2 * P:3 * P],
                                                   kr[:, i].rearrange("p n d -> p (n d)"), ident[:]))
                c.free = [done]
                act.wait(done)
                for n, dst in enumerate((ckvt, cq, krot)):
                    hi = act.do(lambda q, n=n, dst=dst: q.activation(
                        dst[:, 0, cols], bank.ap[:, n * P:(n + 1) * P], ACT.Copy))
                dve.wait(hi)
                for n, dst, rows in ((0, ckvt, P), (1, cq, P), (2, krot, DR)):
                    lo = dve.do(lambda q, n=n, dst=dst, rows=rows: q.tensor_tensor(
                        dst[0:rows, 1, cols], bank.ap[0:rows, n * P:(n + 1) * P],
                        dst[0:rows, 0, cols].bitcast(F32), ALU.subtract))
                bank.free = [lo]

            zeroed = pool.do(lambda q: q.memset(krot[DR:P, 1, :].bitcast(F32), 0.0))
            pool.wait(zeroed)
            held = None
            for t in range(NT):
                now = project(t)
                if held:
                    turn(*held)
                held = now
            xnt_read = Ticket(pe.sem, now[3])

            H2 = SEQ // 2
            GROUPS = [[(0, 0, H2)], [(0, H2, H2)], [(1, P, P), (3, 3 * P, P)], [(1, H2, H2)], [(2, H2, H2)]]
            assert len(GROUPS) == NG
            at = [0]

            def carve(n):
                at[0] += n
                return store_b[:, at[0] - n:at[0]]

            qc = Slot(carve(4 * SEQ).rearrange("p (s h t) -> p s h t", s=2, h=2))
            qr = Slot(carve(2 * SEQ).rearrange("p (h t) -> p h t", h=2))
            ph_slots = [Slot(carve(BANK)) for _ in range(NG)]
            pl_slots = [Slot(carve(BANK)) for _ in range(NG)]
            o_slot = Slot(carve(4 * SEQ).rearrange("p (s n h t) -> p s n h t", s=2, n=2, h=2))
            m_slots = [carve(2 * 2 * P).rearrange("p (h s l) -> p h s l", h=2, s=2) for _ in range(2)]
            v_slots = [carve(2 * 2 * D).rearrange("p (h s d) -> p h s d", h=2, s=2) for _ in range(2)]
            wr_slots = [carve(2 * 2 * P).rearrange("p (s m f) -> p s m f", s=2, m=2) for _ in range(2)]

            sum_a = tile(ctx, "sum_a", [P, 2, P])
            sum_b = tile(ctx, "sum_b", [P, 2, H2])
            rot_cos = tile(ctx, "rot_cos", [P, SEQ])
            rot_sin = tile(ctx, "rot_sin", [P, SEQ])
            rot = tile(ctx, "rot", [P, SEQ])
            cos_t = tile(ctx, "cos_t", [P, SEQ])
            sin_t = tile(ctx, "sin_t", [P, SEQ])
            raw = tile(ctx, "raw", [P, 2, 3 * P + D])
            raw_wr = tile(ctx, "raw_wr", [P, 2, P])
            ones = tile(ctx, "ones", [P, 1])
            inv_store = tile(ctx, "inv_store", [P, 2, 2 * TB])
            p_ring = Ring([Slot(p_store[:, i, :]) for i in range(NG + 1)])
            inv_ring = Ring([Slot(inv_store[:, i, :]) for i in range(2)])
            sums = Slot(None)
            rotary = Slot(None)

            const_in = [Stream(sem(ctx, f"const_in{n}")) for n in range(2)]
            raw_in = [Stream(sem(ctx, f"raw_in{n}_{i}")) for n in range(2) for i in range(4)]
            wr_in = [Stream(sem(ctx, f"wr_in{n}")) for n in range(2)]
            out_sem = [Stream(sem(ctx, f"out_sent{b}")) for b in range(NB)]

            ones_made = pool.do(lambda q: q.memset(ones[:], 1.0))
            cos_here = const_in[0].start(sp, cos_t[:], rope_cos_t)
            sin_here = const_in[1].start(sp, sin_t[:], rope_sin_t)

            bank_ring = Ring(bank_slots[0:6])
            o_banks = bank_slots[6:8]
            raw_free = [[], []]
            W = {}

            def split_bank(done, bank, hi_out, lo_out, src):
                act.wait(done)
                hi = act.do(lambda q: q.activation(hi_out, src, ACT.Copy))
                dve.wait(hi)
                lo = dve.do(lambda q: q.tensor_tensor(lo_out, src, hi_out.bitcast(F32), ALU.subtract))
                bank.free = [lo]
                return lo

            def head_weights(p, h):
                rows = slice((2 * p + h) * P, (2 * p + h + 1) * P)
                sp.wait(*raw_free[h])
                got = [raw_in[4 * h + j].start(sp, raw[:, h, a:a + w], src[rows, :]) for j, (a, w, src) in
                       enumerate(((0, P, wuq), (P, P, wuk), (2 * P, P, wuv), (3 * P, D, wot)))]
                ready = []
                for dst, a, b, w in ((m_slots[p % 2][:, h], 0, P, P), (v_slots[p % 2][:, h], 2 * P, 3 * P, D)):
                    bank = bank_ring.next()
                    pe.wait(*got, *bank.free)
                    done = pe.do(lambda q, a=a, b=b, w=w, bank=bank: q.matmul(
                        bank.ap[:, 0:w], raw[:, h, a:a + P], raw[:, h, b:b + w], start=True, stop=True))
                    ready.append(split_bank(done, bank, dst[:, 0, :], dst[:, 1, :], bank.ap[:, 0:w]))
                raw_free[h] = [done]
                W[p, h] = ready

            def rotary_weights(p):
                cols = slice(p * P, (p + 1) * P)
                sp.wait(*wr_free)
                got = [wr_in[m].start(sp, raw_wr[:, m, :], src[:, cols])
                       for m, src in enumerate((wqrt, wqrt_swapped))]
                dst = wr_slots[p % 2]
                act.wait(*got, *wr_read[p % 2])
                hi = act.do(lambda q: q.activation(dst[:, 0], raw_wr[:], ACT.Copy))
                dve.wait(hi)
                lo = dve.do(lambda q: q.tensor_tensor(dst[:, 1], raw_wr[:], dst[:, 0].bitcast(F32), ALU.subtract))
                wr_free[:] = [lo]
                W[p, "wr"] = lo

            wr_free, wr_read = [], {0: [], 1: []}

            def rotate(p, b):
                toks = slice(b * SEQ, (b + 1) * SEQ)
                w = wr_slots[p % 2]
                done = []
                two = [bank_ring.next(), bank_ring.next()]
                for m, bank in enumerate(two):
                    pe.wait(W[p, "wr"], *bank.free)
                    done.append(product(pe, bank.ap, split3(w[:, 0, m, :], w[:, 1, m, :],
                                                            cq[:, 0, toks], cq[:, 1, toks])))
                wr_read[p % 2] = [done[1]]
                dve.wait(cos_here, sin_here, done[0], *rotary.free)
                two[0].free = [dve.do(lambda q: q.tensor_tensor(rot_cos[:], two[0].ap, cos_t[:], ALU.mult))]
                dve.wait(done[1])
                two[1].free = [dve.do(lambda q: q.tensor_tensor(rot_sin[:], two[1].ap, sin_t[:], ALU.mult))]
                pool.wait(*two[1].free)
                turned = pool.do(lambda q: q.tensor_tensor(rot[:], rot_cos[:], rot_sin[:], ALU.add))
                return turned

            def rotate_high(turned):
                up, dn = slice(0, DR), slice(DR, P)
                act.wait(turned, *qr.free)
                act.do(lambda q: q.activation(qr.ap[up, 0, :], rot[up, :], ACT.Copy))
                act.do(lambda q: q.activation(qr.ap[dn, 1, :], rot[dn, :], ACT.Copy))
                hi = act.do(lambda q: q.activation(qr.ap[up, 1, :], rot[dn, :], ACT.Copy))
                dve.wait(hi)
                dve.do(lambda q: q.tensor_tensor(qr.ap[dn, 0, :], rot[up, :], qr.ap[up, 0, :].bitcast(F32),
                                                 ALU.subtract))
                lo = dve.do(lambda q: q.tensor_tensor(qr.ap[dn, 1, :], rot[dn, :], qr.ap[dn, 1, :].bitcast(F32),
                                                      ALU.subtract))
                rotary.free = [lo]
                qr.ready = [lo]

            def queries(p, b):
                toks = slice(b * SEQ, (b + 1) * SEQ)
                m = m_slots[p % 2]
                act_wait = list(qc.free)
                for h in range(2):
                    bank = bank_ring.next()
                    pe.wait(W[p, h][0], *bank.free)
                    done = product(pe, bank.ap, split3(m[:, h, 0, :], m[:, h, 1, :], cq[:, 0, toks], cq[:, 1, toks]))
                    act.wait(*act_wait)
                    qc.ready = [split_bank(done, bank, qc.ap[:, 0, h, :], qc.ap[:, 1, h, :], bank.ap)]

            def scores(b):
                pe.wait(*qc.ready, *qr.ready)
                weights, low = [], []

                def take_low(g):
                    w, hi = weights[g][0], weights[g][1]
                    eng = dve
                    eng.wait(hi, *pl_slots[g].free)
                    low.append(eng.do(lambda q: q.tensor_tensor(
                        pl_slots[g].ap, w.ap, ph_slots[g].ap.bitcast(F32), ALU.subtract)))

                for g, pieces in enumerate(GROUPS):
                    bank, w, ph = bank_ring.next(), p_ring.next(), ph_slots[g]
                    pe.wait(*bank.free)
                    off = 0
                    for k, q0, n in pieces:
                        keys = slice(b * SEQ + k * P, b * SEQ + (k + 1) * P)
                        toks = slice(q0, q0 + n)
                        pairs = split3(ckvt[:, 0, keys], ckvt[:, 1, keys], qc.ap[:, 0, :, toks], qc.ap[:, 1, :, toks])
                        pairs += [(krot[:, 0, keys], qr.ap[:, :, toks]), (krot[:, 1, keys], qr.ap[:, :, toks])]
                        done = product(pe, bank.ap[:, off:off + 2 * n].rearrange("p (h t) -> p h t", h=2), pairs)
                        off += 2 * n
                    act.wait(done, *w.free)
                    exps = act.do(lambda q, w=w, bank=bank: q.activation(w.ap, bank.ap, ACT.Exp, scale=SCALE))
                    bank.free = [exps]
                    if g >= 1:
                        round_high(g - 1, weights)
                    dve.wait(exps)
                    ready = dve.do(lambda q, w=w: q.tensor_scalar(
                        w.ap, w.ap, float(np.exp(-CLIP * SCALE)), float(np.exp(CLIP * SCALE)), ALU.max, ALU.min))
                    if g in (0, 2, 4):
                        pool.wait(ready)
                        part = (w.ap.rearrange("p (h t) -> p h t", t=P) if g == 2
                                else w.ap.rearrange("p (h t) -> p h t", h=2)[:, :, 0:P])
                        ready = pool.do(lambda q, part=part, n=4 if g == 2 else 2: q.affine_select(
                            out=part, in_=part, compare_op=ALU.is_ge, fill=0.0, base=0,
                            pattern=[[0, n], [1, P]], channel_multiplier=-1))
                    weights.append([w, ready])
                    if g >= 2:
                        take_low(g - 2)
                qc.free = qr.free = [done]
                round_high(NG - 1, weights)
                return weights, low, take_low

            masked_at = {}

            def round_high(g, weights):
                w, ready = weights[g]
                act.wait(ready, *ph_slots[g].free)
                masked_at[g] = ready
                weights[g][1] = act.do(lambda q: q.activation(ph_slots[g].ap, w.ap, ACT.Copy))

            def add_up(weights):
                w = [x[0].ap.rearrange("p (h t) -> p h t", h=2) for x in weights]
                w1_q1 = weights[2][0].ap[:, 0:2 * P].rearrange("p (h t) -> p h t", h=2)
                w3_q3 = weights[2][0].ap[:, 2 * P:4 * P].rearrange("p (h t) -> p h t", h=2)
                pool.wait(masked_at[0], masked_at[1], masked_at[2], masked_at[3], masked_at[4], *sums.free)
                pool.do(lambda q: q.tensor_tensor(sum_a[:], w[0][:, :, P:2 * P], w1_q1, ALU.add))
                t = pool.do(lambda q: q.tensor_tensor(sum_b[:], w[1], w[3], ALU.add))
                pool.wait(t)
                t = pool.do(lambda q: q.tensor_tensor(sum_b[:], sum_b[:], w[4], ALU.add))
                pool.wait(t)
                return pool.do(lambda q: q.tensor_tensor(sum_b[:, :, P:2 * P], sum_b[:, :, P:2 * P], w3_q3, ALU.add))

            def attend(b, weights, low, summed):
                whole_bank, second = (0, H2), (P, H2)
                plan = [[(0, 0, 0, whole_bank), (2, 0, 1, second)],
                        [(1, 0, 0, whole_bank), (3, 0, 1, whole_bank), (4, 0, 2, whole_bank), (2, 2 * P, 3, second)]]
                reads = []
                for n, steps in enumerate(plan):
                    bank = o_banks[n]
                    pe.wait(*bank.free)
                    for j, (g, a, k, (c0, c1)) in enumerate(steps):
                        t = b * TB + k
                        width = c1 - c0
                        pe.wait(low[g])
                        dst = bank.ap.rearrange("p (h t) -> p h t", h=2)[:, :, c0:c1]
                        hi, lo = (s[g].ap[:, a:a + 2 * width].rearrange("p (h t) -> p h t", h=2)
                                  for s in (ph_slots, pl_slots))
                        done = product(pe, dst, split3(ckv[:, 0, t, :], ckv[:, 1, t, :], hi, lo),
                                       first=j == 0, last=j == len(steps) - 1)
                    reads.append(done)
                for s in ph_slots + pl_slots:
                    s.free = [done]
                bank, inv = bank_ring.next(), inv_ring.next()
                pe.wait(summed, ones_made, *bank.free)
                first = weights[0][0].ap.rearrange("p (h t) -> p h t", h=2)
                for h in range(2):
                    src = [first[:, h, 0:P], sum_a[:, h, :], sum_b[:, h, 0:P], sum_b[:, h, P:2 * P]]
                    for t in range(TB):
                        dens = pe.do(lambda q, c=h * TB + t, src=src[t], bank=bank: q.matmul(
                            bank.ap[:, c:c + 1], src, ones[:], start=True, stop=True))
                sums.free = [dens]
                for x, _ in weights:
                    x.free = [dens, *low]
                o_ready = []
                for n in range(2):
                    act.wait(*o_slot.free)
                    o_ready.append(split_bank(reads[n], o_banks[n], o_slot.ap[:, 0, n], o_slot.ap[:, 1, n],
                                              o_banks[n].ap.rearrange("p (h t) -> p h t", h=2)))
                dve.wait(dens, *inv.free)
                inverted = dve.do(lambda q: q.reciprocal(inv.ap, bank.ap[:, 0:2 * TB]))
                bank.free = [inverted]
                return o_ready, inv, inverted

            def output(p, b, o_ready, inv, inverted, between=()):
                between = dict(between)
                v = v_slots[p % 2]
                for tt in range(TB):
                    for h in range(2):
                        y = bank_ring.next()
                        n, c0 = tt // 2, tt % 2 * P
                        o = o_slot.ap[:, :, n, h, c0:c0 + P]
                        pe.wait(o_ready[n], W[p, h][1], *y.free)
                        done = product(pe, y.ap, split3(o[:, 0], o[:, 1], v[:, h, 0, :], v[:, h, 1, :]))
                        t = b * TB + tt
                        dve.wait(done, inverted, acc_done.get(t))
                        y_read = dve.do(lambda q, y=y, t=t, c=h * TB + tt: q.scalar_tensor_tensor(
                            acc[:, t, :], y.ap, inv.ap[:, c:c + 1], acc[:, t, :], ALU.mult, ALU.add))
                        y.free = [y_read]
                        acc_done[t] = y_read
                        if 2 * tt + h in between:
                            between[2 * tt + h]()
                o_slot.free = [done]
                inv.free = [y_read]
                if p == PAIRS - 1:
                    sp.wait(y_read)
                    sent.append(out_sem[b].start(sp, out_t[:, b * TB:(b + 1) * TB, :],
                                                 acc[:, b * TB:(b + 1) * TB, :]))

            sent = []
            units = [(p, b) for p in range(PAIRS) for b in range(NB)]
            for queue in (act, dve, pool):
                queue.wait(xnt_read)
            rotary_weights(0)
            head_weights(0, 0)
            head_weights(0, 1)
            turn(*held)
            for s in p_ring.slots:
                s.free = all_done()
            queries(0, 0)
            rotate_high(rotate(0, 0))
            before = None
            for i, (p, b) in enumerate(units):
                after = units[i + 1] if i + 1 < len(units) else None
                weights, low, take_low = scores(b)
                if after:
                    queries(*after)
                    turned = rotate(*after)
                summed = add_up(weights)
                rest = [(1, lambda: take_low(NG - 2)), (2, lambda: take_low(NG - 1))]
                if after:
                    rest.append((5, lambda: rotate_high(turned)))
                if before:
                    output(*before, between=rest)
                else:
                    for _, step in rest:
                        step()
                if b == 1 and p + 1 < PAIRS:
                    rotary_weights(p + 1)
                    head_weights(p + 1, 0)
                if b == 2 and p + 1 < PAIRS:
                    head_weights(p + 1, 1)
                before = (p, b, *attend(b, weights, low, summed))
            output(*before)
            sp.wait(*sent)

            with nc.Block() as block:
                block.sync(lambda eng: sp.run(eng))
                block.gpsimd(lambda eng: pool.run(eng))
                block.scalar(lambda eng: act.run(eng))
                block.vector(lambda eng: dve.run(eng))
                block.tensor(lambda eng: pe.run(eng))


def rope_tables(seq, width, tile):
    inv_freq = (np.float32(10000.0) ** (-np.arange(0, width, 2, dtype=np.float32) / np.float32(width)))
    ang = np.arange(seq, dtype=np.float32)[:, None] * inv_freq.astype(np.float32)[None, :]
    c, s = np.cos(ang).astype(np.float32), np.sin(ang).astype(np.float32)
    cos = np.concatenate([c, c, c, c], axis=1).reshape(seq // tile, tile, 2 * width)
    sin = np.concatenate([-s, s, -s, s], axis=1).reshape(seq // tile, tile, 2 * width)
    cos_t, sin_t = (v.reshape(seq, 2 * width).T for v in (cos, sin))
    return cos.transpose(1, 0, 2), sin.transpose(1, 0, 2), cos_t, sin_t


def kernel(**inputs):
    import concourse.bacc as bacc
    from concourse.bass_utils import run_bass_kernel_spmd

    att, ffn = "L0_attn_", "L0_ffn_"
    a = {n: np.asarray(v) for n, v in inputs.items()}
    d_rot = a[att + "W_KR"].shape[0]
    heads = a[att + "W_QR"].shape[0] // d_rot
    wqr = a[att + "W_QR"].reshape(heads, d_rot // 2, 2, -1).transpose(0, 2, 1, 3).reshape(heads * d_rot, -1)
    wkr = a[att + "W_KR"].reshape(d_rot // 2, 2, -1).transpose(1, 0, 2).reshape(d_rot, -1)
    halves = a[att + "W_QR"].shape[0] // d_rot, 2, d_rot // 2
    wqr_swapped = wqr.reshape(*halves, -1)[:, ::-1].reshape(heads * d_rot, -1)
    cos, sin, cos_t, sin_t = rope_tables(a[att + "x"].shape[1], d_rot, 128)
    laid = {
        "x": a[att + "x"], "wdqt": a[att + "W_DQ"].T, "wuq": a[att + "W_UQ"], "wqrt": wqr.T, "wqrt_swapped": wqr_swapped.T,
        "wdkvt": a[att + "W_DKV"].T, "wuk": a[att + "W_UK"], "wuv": a[att + "W_UV"], "wkrt": wkr.T,
        "wot": a[att + "W_O"].T,
        "w1": a[ffn + "W1"], "wg": a[ffn + "Wg"], "w2": a[ffn + "W2"],
        "ws1": a[ffn + "Ws1"], "wsg": a[ffn + "Wsg"], "ws2": a[ffn + "Ws2"],
        "gate_w": a[ffn + "gate_w"], "gate_b": a[ffn + "gate_b"], "biases": a[ffn + "biases"],
        "rope_cos": cos, "rope_sin": sin, "rope_cos_t": cos_t, "rope_sin_t": sin_t,
    }
    nc = bacc.Bacc("TRN2", target_bir_lowering=False, num_devices=1)
    arrays, args = {}, []
    for name, v in laid.items():
        arrays[f"in_{name}"] = np.ascontiguousarray(v)
        args.append(nc.dram_tensor(f"in_{name}", v.shape, F32, kind="ExternalInput").ap())
    args.append(nc.dram_tensor("out_0", a[att + "x"].shape, F32, kind="ExternalOutput").ap())
    program(nc, *args)
    r = run_bass_kernel_spmd(nc, [arrays], core_ids=[0])
    return r.results[0]["out_0"]
```

```python
from contextlib import ExitStack

import numpy as np

import concourse.bass as bass
from concourse import mybir

ALU = mybir.AluOpType
ACT = mybir.ActivationFunctionType
AX = mybir.AxisListType
F32 = mybir.dt.float32
F32R = mybir.dt.float32r

P = 128
BANK = 512
LN_EPS = 1e-5
TOP_K = 3
CLIP = 80.0


class Ticket:

    def __init__(self, sem, value):
        self.sem, self.value = sem, value


class Queue:

    def __init__(self, sem):
        self.sem, self.steps, self.count, self.waited = sem, [], 0, {}

    def wait(self, *tickets):
        for t in tickets:
            if t is None or self.waited.get(id(t.sem), 0) >= t.value:
                continue
            self.waited[id(t.sem)] = t.value
            self.steps.append(lambda eng, t=t: eng.wait_ge(t.sem, t.value))

    def do(self, make):
        self.count += 1
        self.steps.append(lambda eng: make(eng).then_inc(self.sem, 1))
        return Ticket(self.sem, self.count)

    def quiet(self, make):
        self.steps.append(lambda eng: make(eng))

    def run(self, eng):
        for step in self.steps:
            step(eng)


class Stream:

    def __init__(self, sem):
        self.sem, self.count = sem, 0

    def start(self, queue, out, in_):
        self.count += 16
        queue.steps.append(lambda eng: eng.dma_start(out, in_).then_inc(self.sem, 16))
        return Ticket(self.sem, self.count)


class Slot:

    def __init__(self, ap):
        self.ap, self.free, self.ready = ap, [], []


class Ring:
    def __init__(self, slots):
        self.slots, self.at = slots, 0

    def next(self):
        s = self.slots[self.at % len(self.slots)]
        self.at += 1
        return s


def product(pe, out, pairs, first=True, last=True):
    t = None
    for n, (a, b) in enumerate(pairs):
        start, stop = first and n == 0, last and n == len(pairs) - 1
        make = lambda eng, a=a, b=b, start=start, stop=stop: eng.matmul(out, a, b, start=start, stop=stop)
        if n == len(pairs) - 1:
            t = pe.do(make)
        else:
            pe.quiet(make)
    return t


def split3(a_hi, a_lo, b_hi, b_lo):
    return [(a_hi, b_hi), (a_hi, b_lo), (a_lo, b_hi)]


def program(nc, x, wdqt, wuq, wqrt, wdkvt, wuk, wuv, wkrt, wot, w1, wg, w2, ws1, wsg, ws2,
            gate_w, gate_b, biases, rope_cos, rope_sin, rope_cos_t, rope_sin_t, out):
    BATCH, SEQ, D = x.shape
    TOK = BATCH * SEQ
    NT = TOK // P
    NB = TOK // BANK
    TB = BANK // P
    NE, _, HID = w1.shape
    DC, HC = D // P, HID // P
    LAT = wdqt.shape[1]
    DR = wkrt.shape[1]
    HEADS = wuq.shape[0] // P
    PAIRS = HEADS // 2
    DH = wuq.shape[0] // HEADS
    SCALE = float(1.0 / np.sqrt(np.float32(DH + DR)))
    assert SEQ == BANK and LAT == P and 2 * DR == P and DH == P and D == BANK

    x_t = x.rearrange("b (t p) d -> p (b t) d", p=P)
    out_t = out.rearrange("b (t p) d -> p (b t) d", p=P)

    with ExitStack() as whole:
        def tile(ctx, name, shape, dt=F32):
            return ctx.enter_context(nc.sbuf_tensor(name, shape, dt))

        def sem(ctx, name):
            return ctx.enter_context(nc.semaphore(name))

        pe, act, dve, pool = (Queue(sem(whole, f"{n}_done")) for n in ("pe", "act", "dve", "pool"))
        sp = Queue(None)

        def all_done():
            return [Ticket(q.sem, q.count) for q in (pe, act, dve, pool)]

        bank_slots = [Slot(whole.enter_context(nc.psum_tensor(f"bank{i}", [P, BANK], F32))[:]) for i in range(8)]

        acc = tile(whole, "acc", [P, NT, D])
        store_a = tile(whole, "store_a", [P, 16384], F32R)
        store_b = tile(whole, "store_b", [P, 16384], F32R)
        ident = tile(whole, "ident", [P, P])
        WC = 2 * LAT + DR
        w_cat = tile(whole, "w_cat", [P, 2, DC, WC], F32R)
        acc_done = {}

        xnt = store_b[:].rearrange("p (s c t) -> p s c t", s=2, c=DC)
        xnt_hi, xnt_lo = xnt[:, 0], xnt[:, 1]

        with ExitStack() as ctx:
            UPS, DNS = 5, 6
            up_w = store_a[:, 0:UPS * 2048].rearrange("p (n s m c h) -> p n s m c h", n=UPS, s=2, m=2, c=DC)
            dn_w = store_a[:, UPS * 2048:UPS * 2048 + DNS * 1024].rearrange("p (n s d) -> p n s d", n=DNS, s=2)
            up_slots = [Slot(up_w[:, n]) for n in range(UPS)]
            dn_slots = [Slot(dn_w[:, n]) for n in range(DNS)]
            raw_up = tile(ctx, "raw_up", [P, 2, 2, DC, P])
            raw_dn = tile(ctx, "raw_dn", [P, 2, D])
            g_store = tile(ctx, "g_store", [P, 2, 2, BANK], F32R)
            s_store = tile(ctx, "s_store", [P, 2, BANK])
            h_store = tile(ctx, "h_store", [P, 2, BANK])
            stats = tile(ctx, "stats", [P, NT, 6])
            mv = tile(ctx, "mv", [P, NT, 2])
            var_eps = tile(ctx, "var_eps", [P, NT])
            rstd = tile(ctx, "rstd", [P, NT])
            neg_half = tile(ctx, "neg_half", [P, NT])
            gw_raw = tile(ctx, "gw_raw", [P, DC, 8])
            gw = tile(ctx, "gw", [P, DC, 16], F32R)
            gb = tile(ctx, "gb", [P, 8])
            eb = tile(ctx, "eb", [P, 8])
            logit = tile(ctx, "logit", [P, NT, 8])
            prob = tile(ctx, "prob", [P, NT, 8])
            biased = tile(ctx, "biased", [P, NT, 8])
            beats = tile(ctx, "beats", [P, NT, 8])
            rank = tile(ctx, "rank", [P, NT, 8])
            chosen = tile(ctx, "chosen", [P, NT, 8])
            share = tile(ctx, "share", [P, NT, 8])
            col = tile(ctx, "col", [P, NT, 2])

            x_in = [Stream(sem(ctx, f"x_in{t}")) for t in range(NT)]
            gate_in = Stream(sem(ctx, "gate_in"))
            wu_in = [Stream(sem(ctx, f"wu_in{n}")) for n in range(2)]
            wg_in = [Stream(sem(ctx, f"wg_in{n}")) for n in range(2)]
            wd_in = [Stream(sem(ctx, f"wd_in{n}")) for n in range(2)]
            cat_in = [Stream(sem(ctx, f"cat_in{n}")) for n in range(3)]

            x_here = {}

            def load_x(b):
                for t in range(b * TB, (b + 1) * TB):
                    x_here[t] = x_in[t].start(sp, acc[:, t, :], x_t[:, t, :])

            t = pool.do(lambda e: e.memset(ident[:], 0.0))
            pool.wait(t)
            ident_made = pool.do(lambda e: e.affine_select(
                out=ident[:], in_=ident[:], compare_op=ALU.not_equal, fill=1.0, base=0,
                pattern=[[-1, P]], channel_multiplier=1))
            half_made = pool.do(lambda e: e.memset(neg_half[:], -0.5))
            pad_made = pool.do(lambda e: e.memset(gw_raw[:], 0.0))

            up_ring = Ring(bank_slots[0:4])
            y_slots = bank_slots[4:8]
            s_ring = Ring([Slot(s_store[:, i, :]) for i in range(2)])

            def statistics(b):
                tiles = range(b * TB, (b + 1) * TB)
                for t in tiles:
                    dve.wait(x_here[t])
                    got = dve.do(lambda e, t=t: e.bn_stats(out=stats[:, t, :], in_=acc[:, t, :]))
                dve.wait(got)
                for t in tiles:
                    got = dve.do(lambda e, t=t: e.bn_aggr(out=mv[:, t, :], in_=stats[:, t, :]))
                dve.wait(got)
                var_ready = dve.do(lambda e: e.tensor_scalar(
                    var_eps[:, b * TB:(b + 1) * TB], mv[:, b * TB:(b + 1) * TB, 1], LN_EPS, None, ALU.add))
                pool.wait(var_ready, half_made)
                rstd_ready[b] = pool.do(lambda e: e.tensor_tensor(
                    rstd[:, b * TB:(b + 1) * TB], var_eps[:, b * TB:(b + 1) * TB],
                    neg_half[:, b * TB:(b + 1) * TB], ALU.pow))

            rstd_ready, xnt_ready = {}, {}

            def normalise(t):
                xn = s_ring.next()
                dve.wait(rstd_ready[t // TB], *xn.free)
                xn_ready = dve.do(lambda e: e.tensor_scalar(
                    xn.ap, acc[:, t, :], mv[:, t, 0:1], rstd[:, t:t + 1], ALU.subtract, ALU.mult))
                return t, xn, xn_ready

            def turn_rows(t, xn, xn_ready):
                bank = up_ring.next()
                pe.wait(xn_ready, ident_made, *bank.free)
                for c in range(DC):
                    turned = pe.do(lambda e, c=c: e.transpose(
                        bank.ap[:, c * P:(c + 1) * P], xn.ap[:, c * P:(c + 1) * P], ident[:]))
                xn.free = [turned]
                src = bank.ap.rearrange("p (c t) -> p c t", c=DC)
                cols = slice(t * P, (t + 1) * P)
                act.wait(turned)
                hi = act.do(lambda e: e.activation(xnt_hi[:, :, cols], src, ACT.Copy))
                dve.wait(hi)
                lo = dve.do(lambda e: e.tensor_tensor(
                    xnt_lo[:, :, cols], src, xnt_hi[:, :, cols].bitcast(F32), ALU.subtract))
                bank.free = [lo]
                xnt_ready[t // TB] = lo

            def load_weights(k):
                e, hc = divmod(k, HC)
                r = k % 2
                src1, srcg, src2 = (ws1, wsg, ws2) if e == 0 else (w1[e - 1], wg[e - 1], w2[e - 1])
                cols = slice(hc * P, (hc + 1) * P)
                sp.wait(*raw_free[r])
                a = wu_in[r].start(sp, raw_up[:, r, 0], src1.rearrange("(c p) h -> p c h", p=P)[:, :, cols])
                b = wg_in[r].start(sp, raw_up[:, r, 1], srcg.rearrange("(c p) h -> p c h", p=P)[:, :, cols])
                c = wd_in[r].start(sp, raw_dn[:, r], src2[cols, :])
                up, dn = up_slots[k % UPS], dn_slots[k % DNS]
                act.wait(a, b, *up.free)
                up_hi = act.do(lambda g: g.activation(up.ap[:, 0], raw_up[:, r], ACT.Copy))
                act.wait(c, *dn.free)
                dn_hi = act.do(lambda g: g.activation(dn.ap[:, 0], raw_dn[:, r], ACT.Copy))
                rest = pool
                rest.wait(up_hi)
                up_lo = rest.do(lambda g: g.tensor_tensor(
                    up.ap[:, 1], raw_up[:, r], up.ap[:, 0].bitcast(F32), ALU.subtract))
                rest.wait(dn_hi)
                dn_lo = rest.do(lambda g: g.tensor_tensor(
                    dn.ap[:, 1], raw_dn[:, r], dn.ap[:, 0].bitcast(F32), ALU.subtract))
                raw_free[r] = [dn_lo]
                weights[k] = (up.ap, dn.ap, up_lo, dn_lo)

            raw_free = {0: [], 1: []}
            weights = {}
            g_ring = Ring([Slot(g_store[:, i]) for i in range(2)])
            h_ring = Ring([Slot(h_store[:, i, :]) for i in range(2)])

            def up(e, tb, hc):
                k = e * HC + hc
                w, _, w_ready, _ = weights[k]
                toks = slice(tb * BANK, (tb + 1) * BANK)
                bank1, bankg = up_ring.next(), up_ring.next()
                done = []
                for m, bank in ((0, bank1), (1, bankg)):
                    pe.wait(w_ready, xnt_ready[tb], *bank.free)
                    pairs = []
                    for c in range(DC):
                        pairs += split3(w[:, 0, m, c, :], w[:, 1, m, c, :],
                                        xnt_hi[:, c, toks], xnt_lo[:, c, toks])
                    done.append(product(pe, bank.ap, pairs))
                if tb == NB - 1:
                    up_slots[k % UPS].free = [done[1]]
                s, h, g = s_ring.next(), h_ring.next(), g_ring.next()
                act.wait(done[0], *s.free)
                s_ready = act.do(lambda q: q.activation(s.ap, bank1.ap, ACT.Silu))
                bank1.free = [s_ready]
                dve.wait(s_ready, done[1], *h.free)
                h_ready = dve.do(lambda q: q.tensor_tensor(h.ap, bankg.ap, s.ap, ALU.mult))
                bankg.free = [h_ready]
                s.free = [h_ready]
                act.wait(h_ready, *g.free)
                hi = act.do(lambda q: q.activation(g.ap[:, 0], h.ap, ACT.Copy))
                dve.wait(hi)
                lo = dve.do(lambda q: q.tensor_tensor(g.ap[:, 1], h.ap, g.ap[:, 0].bitcast(F32), ALU.subtract))
                h.free = [lo]
                return g, lo

            def down(e, tb, hc, g, g_ready):
                k = e * HC + hc
                _, w, _, w_ready = weights[k]
                pe.wait(g_ready, w_ready)
                for tt in range(TB):
                    y = y_slots[tt]
                    if hc == 0:
                        pe.wait(*y.free)
                    cols = slice(tt * P, (tt + 1) * P)
                    done = product(pe, y.ap, split3(g.ap[:, 0, cols], g.ap[:, 1, cols], w[:, 0], w[:, 1]),
                                   first=hc == 0, last=hc == HC - 1)
                    if hc == HC - 1:
                        t = tb * TB + tt
                        dve.wait(done, acc_done.get(t))
                        if e == 0:
                            y_read = dve.do(lambda q, y=y, t=t: q.tensor_tensor(
                                acc[:, t, :], y.ap, acc[:, t, :], ALU.add))
                        else:
                            dve.wait(*share_ready)
                            y_read = dve.do(lambda q, y=y, t=t: q.scalar_tensor_tensor(
                                acc[:, t, :], y.ap, share[:, t, e - 1:e], acc[:, t, :], ALU.mult, ALU.add))
                        y.free = [y_read]
                        acc_done[t] = y_read
                g.free = [done]
                if tb == NB - 1:
                    dn_slots[k % DNS].free = [done]

            share_ready, gate_steps = [], []

            def gate_weights():
                act.wait(gate_here[0])
                gw_hi = act.do(lambda q: q.activation(gw[:, :, 0:8], gw_raw[:], ACT.Copy))
                dve.wait(gw_hi)
                return dve.do(lambda q: q.tensor_tensor(gw[:, :, 8:16], gw_raw[:], gw[:, :, 0:8].bitcast(F32),
                                                        ALU.subtract))

            def gate(gw_ready):
                back = up_ring.next()
                pe.wait(gw_ready, xnt_ready[NB - 1])
                pe.wait(*back.free)

                def logits(b):
                    bank, rows = up_ring.next(), h_ring.next()
                    if bank is back:
                        bank = up_ring.next()
                    toks = slice(b * BANK, (b + 1) * BANK)
                    pe.wait(*bank.free)
                    product(pe, bank.ap[0:16, :], [(gw[:, c, :], xnt_hi[:, c, toks]) for c in range(DC)], last=False)
                    done = product(pe, bank.ap[0:8, :], [(gw[:, c, 0:8], xnt_lo[:, c, toks]) for c in range(DC)],
                                   first=False)
                    act.wait(done, *rows.free)
                    copied = act.do(lambda q: q.activation(rows.ap[0:16, :], bank.ap[0:16, :], ACT.Copy))
                    bank.free = [copied]
                    return b, rows, copied

                def turn_logits(b, rows, copied):
                    pe.wait(copied)
                    for t in range(TB):
                        turned = pe.do(lambda q, t=t: q.transpose(
                            back.ap[:, (b * TB + t) * 16:(b * TB + t + 1) * 16],
                            rows.ap[0:16, t * P:(t + 1) * P], ident[0:16, 0:16]))
                    rows.free = [turned]
                    return turned

                held = logits(0)
                for b in range(1, NB):
                    following = logits(b)
                    turn_logits(*held)
                    held = following
                if pending:
                    down(*pending)
                turned = turn_logits(*held)
                act.wait(turned)
                both = back.ap[:, 0:NT * 16].rearrange("p (t e) -> p t e", e=16)
                got = act.do(lambda q: q.activation(logit[:], both[:, :, 0:8], ACT.Copy))
                dve.wait(got)
                got = dve.do(lambda q: q.tensor_tensor(logit[:], both[:, :, 8:16], logit[:], ALU.add))
                back.free = [got]
                last = [got]

                def chain(make, queue=dve):
                    def step():
                        queue.wait(last[0])
                        last[0] = queue.do(make)
                    gate_steps.append(step)

                ex = slice(0, NE)

                def over(v):
                    return v.unsqueeze(1).broadcast_to([P, NT, NE])

                def spread(v):
                    return v.broadcast_to([P, NT, NE])

                chain(lambda q: q.tensor_tensor(logit[:, :, ex], logit[:, :, ex], over(gb[:, ex]), ALU.add))
                chain(lambda q: q.tensor_reduce(col[:, :, 0], logit[:, :, ex], AX.X, ALU.max))
                chain(lambda q: q.tensor_tensor(logit[:, :, ex], logit[:, :, ex], spread(col[:, :, 0:1]),
                                                ALU.subtract))
                chain(lambda q: q.activation(prob[:, :, ex], logit[:, :, ex], ACT.Exp), act)
                chain(lambda q: q.tensor_reduce(col[:, :, 0], prob[:, :, ex], AX.X, ALU.add))
                chain(lambda q: q.reciprocal(col[:, :, 1], col[:, :, 0]))
                chain(lambda q: q.tensor_tensor(prob[:, :, ex], prob[:, :, ex], spread(col[:, :, 1:2]), ALU.mult))
                chain(lambda q: q.tensor_tensor(biased[:, :, ex], prob[:, :, ex], over(eb[:, ex]), ALU.add))
                for n in range(NE):
                    if n:
                        chain(lambda q, n=n: q.tensor_tensor(
                            beats[:, :, 0:n], biased[:, :, 0:n],
                            biased[:, :, n:n + 1].broadcast_to([P, NT, n]), ALU.is_ge))
                    chain(lambda q, n=n: q.tensor_tensor(
                        beats[:, :, n:NE], biased[:, :, n:NE],
                        biased[:, :, n:n + 1].broadcast_to([P, NT, NE - n]), ALU.is_gt))
                    chain(lambda q, n=n: q.tensor_reduce(rank[:, :, n], beats[:, :, ex], AX.X, ALU.add))
                chain(lambda q: q.tensor_scalar(chosen[:, :, ex], rank[:, :, ex], TOP_K - 0.5, None, ALU.is_lt))
                chain(lambda q: q.tensor_tensor(chosen[:, :, ex], chosen[:, :, ex], prob[:, :, ex], ALU.mult))
                chain(lambda q: q.tensor_reduce(col[:, :, 0], chosen[:, :, ex], AX.X, ALU.add))
                chain(lambda q: q.reciprocal(col[:, :, 1], col[:, :, 0]))
                chain(lambda q: q.tensor_tensor(share[:, :, ex], chosen[:, :, ex], spread(col[:, :, 1:2]), ALU.mult))
                gate_steps.append(lambda: share_ready.append(last[0]))

            gate_here = [None]
            act.wait(pad_made)
            for dst, src in ((gw_raw[:, :, 0:NE], gate_w.rearrange("(c p) e -> p c e", p=P)),
                             (gb[:, 0:NE], gate_b.rearrange("(o e) -> o e", o=1).broadcast_to([P, NE])),
                             (eb[:, 0:NE], biases.rearrange("(o e) -> o e", o=1).broadcast_to([P, NE]))):
                gate_here[0] = gate_in.start(act, dst, src)

            order = [(e, tb, hc) for e in range(NE + 1) for tb in range(NB) for hc in range(HC)]
            NK = (NE + 1) * HC
            GATE_STEPS_A_CHUNK = 8
            AHEAD = TB
            load_x(0)
            statistics(0)
            load_weights(0)
            load_x(1)
            rows = normalise(0)
            for t in range(1, AHEAD):
                following = normalise(t)
                turn_rows(*rows)
                rows = following
            turn_rows(*rows)
            load_weights(1)
            statistics(1)
            loaded = 2
            pending = None
            for e, tb, hc in order:
                t = tb * HC + hc + AHEAD
                rows = None
                if e == 0 and t < NT:
                    rows = normalise(t)
                    if (t + 2) % TB == 0 and t + 2 < NT:
                        statistics((t + 2) // TB)
                g, g_ready = up(e, tb, hc)
                if loaded < HC:
                    load_weights(loaded)
                    load_x(loaded)
                    loaded += 1
                if rows:
                    turn_rows(*rows)
                if e == 0 and tb == NB - 1 and hc == 0:
                    gate(gw_ready)
                elif pending:
                    down(*pending)
                if (e, tb, hc) == (0, 1, 0):
                    gw_ready = gate_weights()
                pending = (e, tb, hc, g, g_ready)
                for step in gate_steps[:GATE_STEPS_A_CHUNK]:
                    step()
                del gate_steps[:GATE_STEPS_A_CHUNK]
                if HC <= loaded < NK and (tb == 1 and hc == 0 or tb == NB - 1 and hc >= 1):
                    load_weights(loaded)
                    loaded += 1
                if (e, tb, hc) == (NE, 1, 0):
                    w_raw = raw_up[:].rearrange("p a b c h -> p (a b c h)")[:, 0:DC * WC].rearrange(
                        "p (c n) -> p c n", c=DC)
                    sp.wait(*raw_free[0], *raw_free[1])
                    here = [cat_in[n].start(sp, w_raw[:, :, a:a + w], src.rearrange("(c p) n -> p c n", p=P))
                            for n, (a, w, src) in enumerate(((0, LAT, wdkvt), (LAT, LAT, wdqt), (2 * LAT, DR, wkrt)))]
                    act.wait(*here)
                    cat_hi = act.do(lambda q: q.activation(w_cat[:, 0], w_raw, ACT.Copy))
                    pool.wait(cat_hi)
                    cat_ready = pool.do(lambda q: q.tensor_tensor(w_cat[:, 1], w_raw, w_cat[:, 0].bitcast(F32),
                                                                  ALU.subtract))
            assert not gate_steps and loaded == NK
            down(*pending)

        lat_a = store_a[:].rearrange("p (n s t) -> p n s t", n=4, s=2)
        cq, ckvt, ckv_flat, krot = (lat_a[:, n] for n in range(4))
        ckv = ckv_flat.rearrange("p s (t l) -> p s t l", l=LAT)

        experts_done = all_done()
        with ExitStack() as ctx:
            NG = 5
            p_store = tile(ctx, "p_store", [P, NG + 1, BANK])
            p_flat = p_store[:].rearrange("p n t -> p (n t)")
            at = [0]

            def carve_small(shape):
                n = int(np.prod(shape))
                at[0] += n
                part = p_flat[:, at[0] - n:at[0]]
                names = "abc"[:len(shape)]
                return part.rearrange(f"p ({' '.join(names)}) -> p {' '.join(names)}", **dict(zip(names, shape)))

            cs, sn = carve_small((TB, P)), carve_small((TB, P))
            c32 = carve_small((2, 2 * LAT))
            kr_cos, kr_sin = carve_small((2, DR)), carve_small((2, DR))
            kr = carve_small((2, 2, DR))
            table_in = [Stream(sem(ctx, f"table_in{n}")) for n in range(2)]
            sp.wait(*experts_done)
            tables_here = [table_in[0].start(sp, cs, rope_cos), table_in[1].start(sp, sn, rope_sin)]
            for queue in (act, dve, pool):
                queue.wait(*experts_done)
            dve.wait(*tables_here)
            ring = Ring(bank_slots)
            c_ring = Ring([Slot(i) for i in range(2)])
            half = DR // 2

            def project(t):
                bank, c = ring.next(), c_ring.next()
                i = c.ap
                cols = slice(t * P, (t + 1) * P)
                pe.wait(cat_ready, *bank.free)
                pairs = []
                for d in range(DC):
                    pairs += split3(xnt_hi[:, d, cols], xnt_lo[:, d, cols], w_cat[:, 0, d, :], w_cat[:, 1, d, :])
                done = product(pe, bank.ap[:, 0:WC], pairs)
                act.wait(done, *c.free)
                act.do(lambda q: q.activation(c32[:, i, :], bank.ap[:, 0:2 * LAT], ACT.Copy))
                hi = act.do(lambda q: q.activation(ckv[:, 0, t, :], bank.ap[:, 0:LAT], ACT.Copy))
                dve.wait(hi, *c.free)
                dve.do(lambda q: q.tensor_tensor(ckv[:, 1, t, :], bank.ap[:, 0:LAT],
                                                 ckv[:, 0, t, :].bitcast(F32), ALU.subtract))
                k1, k2 = (bank.ap[:, 2 * LAT + n * half:2 * LAT + (n + 1) * half] for n in range(2))
                j = t % TB
                dve.do(lambda q: q.tensor_tensor(kr_cos[:, i, :], bank.ap[:, 2 * LAT:WC], cs[:, j, 0:DR], ALU.mult))
                dve.do(lambda q: q.tensor_tensor(kr_sin[:, i, 0:half], k2, sn[:, j, 0:half], ALU.mult))
                read = dve.do(lambda q: q.tensor_tensor(kr_sin[:, i, half:DR], k1, sn[:, j, half:DR], ALU.mult))
                bank.free = [read]
                dve.wait(read)
                for n in range(2):
                    ready = dve.do(lambda q, n=n: q.tensor_tensor(kr[:, i, n, :], kr_cos[:, i, :], kr_sin[:, i, :],
                                                                  ALU.add))
                return t, c, [hi, ready], done.value

            def turn(t, c, ready, _):
                bank, i = ring.next(), c.ap
                cols = slice(t * P, (t + 1) * P)
                pe.wait(*ready, *bank.free)
                pe.quiet(lambda q: q.transpose(bank.ap[:, 0:P], c32[:, i, 0:LAT], ident[:]))
                pe.quiet(lambda q: q.transpose(bank.ap[:, P:2 * P], c32[:, i, LAT:2 * LAT], ident[:]))
                done = pe.do(lambda q: q.transpose(bank.ap[:, 2 * P:3 * P],
                                                   kr[:, i].rearrange("p n d -> p (n d)"), ident[:]))
                c.free = [done]
                act.wait(done)
                for n, dst in enumerate((ckvt, cq, krot)):
                    hi = act.do(lambda q, n=n, dst=dst: q.activation(
                        dst[:, 0, cols], bank.ap[:, n * P:(n + 1) * P], ACT.Copy))
                dve.wait(hi)
                for n, dst, rows in ((0, ckvt, P), (1, cq, P), (2, krot, DR)):
                    lo = dve.do(lambda q, n=n, dst=dst, rows=rows: q.tensor_tensor(
                        dst[0:rows, 1, cols], bank.ap[0:rows, n * P:(n + 1) * P],
                        dst[0:rows, 0, cols].bitcast(F32), ALU.subtract))
                bank.free = [lo]

            zeroed = pool.do(lambda q: q.memset(krot[DR:P, 1, :].bitcast(F32), 0.0))
            pool.wait(zeroed)
            H2 = SEQ // 2
            GROUPS = [[(0, 0, H2)], [(0, H2, H2)], [(1, P, P), (3, 3 * P, P)], [(1, H2, H2)], [(2, H2, H2)]]
            assert len(GROUPS) == NG
            at = [0]

            def carve(n):
                at[0] += n
                return store_b[:, at[0] - n:at[0]]

            qc = Slot(carve(4 * SEQ).rearrange("p (s h t) -> p s h t", s=2, h=2))
            qr = Slot(carve(2 * SEQ).rearrange("p (h t) -> p h t", h=2))
            ph_slots = [Slot(carve(BANK)) for _ in range(NG)]
            pl_slots = [Slot(carve(BANK)) for _ in range(NG)]
            o_slot = Slot(carve(4 * SEQ).rearrange("p (s n h t) -> p s n h t", s=2, n=2, h=2))
            m_slots = [carve(2 * 2 * P).rearrange("p (h s l) -> p h s l", h=2, s=2) for _ in range(2)]
            v_slots = [carve(2 * 2 * D).rearrange("p (h s d) -> p h s d", h=2, s=2) for _ in range(2)]

            sum_b_hi = carve(2 * H2).rearrange("p (h t) -> p h t", h=2)
            sum_b_lo = carve(2 * H2).rearrange("p (h t) -> p h t", h=2)
            sum_a_hi = tile(ctx, "sum_a_hi", [P, 2, P], F32R)
            sum_a_lo = tile(ctx, "sum_a_lo", [P, 2, P], F32R)
            wr_store = tile(ctx, "wr_store", [P, 2, 2, P], F32R)
            wr_slots = [wr_store[:, n] for n in range(2)]
            sum_a = tile(ctx, "sum_a", [P, 2, P])
            sum_b = tile(ctx, "sum_b", [P, 2, H2])
            rot = tile(ctx, "rot", [P, SEQ])
            rot_sin = tile(ctx, "rot_sin", [P, SEQ])
            cos_t = tile(ctx, "cos_t", [P, SEQ])
            sin_t = tile(ctx, "sin_t", [P, SEQ])
            raw = tile(ctx, "raw", [P, 2, 3 * P + D])
            raw_wr = tile(ctx, "raw_wr", [P, P])
            unit = tile(ctx, "unit", [P, 2, 2])
            unit_r = tile(ctx, "unit_r", [P, 2, 2], F32R)
            divisor_rows = tile(ctx, "divisor_rows", [2, BANK])
            inv_store = tile(ctx, "inv_store", [P, 2, 2 * TB])
            p_ring = Ring([Slot(p_store[:, i, :]) for i in range(NG + 1)])
            inv_ring = Ring([Slot(inv_store[:, i, :]) for i in range(2)])
            sums = Slot(None)
            rotary = Slot(None)

            divisor_sent = [Stream(sem(ctx, f"divisor_sent{s}_{n}")) for s in range(2) for n in range(2)]
            const_in = [Stream(sem(ctx, f"const_in{n}")) for n in range(2)]
            raw_in = [Stream(sem(ctx, f"raw_in{n}_{i}")) for n in range(2) for i in range(4)]
            wr_in = Stream(sem(ctx, "wr_in"))
            out_sem = [Stream(sem(ctx, f"out_sent{t}")) for t in range(NT)]

            zeroed = pool.do(lambda q: q.memset(unit[:], 0.0))
            pool.wait(zeroed)
            for s in range(2):
                unit_made = pool.do(lambda q, s=s: q.memset(unit[:, s, s:s + 1], 1.0))
            cos_here = const_in[0].start(sp, cos_t[:], rope_cos_t)
            sin_here = const_in[1].start(sp, sin_t[:], rope_sin_t)

            bank_ring = Ring(bank_slots[0:6])
            o_banks = bank_slots[6:8]
            raw_free = [[], []]
            W = {}

            def split_bank(done, bank, hi_out, lo_out, src):
                act.wait(done)
                hi = act.do(lambda q: q.activation(hi_out, src, ACT.Copy))
                dve.wait(hi)
                lo = dve.do(lambda q: q.tensor_tensor(lo_out, src, hi_out.bitcast(F32), ALU.subtract))
                bank.free = [lo]
                return lo

            def head_weights(p, h):
                rows = slice((2 * p + h) * P, (2 * p + h + 1) * P)
                sp.wait(*raw_free[h])
                got = [raw_in[4 * h + j].start(sp, raw[:, h, a:a + w], src[rows, :]) for j, (a, w, src) in
                       enumerate(((0, P, wuq), (P, P, wuk), (2 * P, P, wuv), (3 * P, D, wot)))]
                ready = []
                for dst, a, b, w in ((m_slots[p % 2][:, h], 0, P, P), (v_slots[p % 2][:, h], 2 * P, 3 * P, D)):
                    bank = bank_ring.next()
                    pe.wait(*got, *bank.free)
                    done = pe.do(lambda q, a=a, b=b, w=w, bank=bank: q.matmul(
                        bank.ap[:, 0:w], raw[:, h, a:a + P], raw[:, h, b:b + w], start=True, stop=True))
                    ready.append(split_bank(done, bank, dst[:, 0, :], dst[:, 1, :], bank.ap[:, 0:w]))
                raw_free[h] = [done]
                W[p, h] = ready

            def rotary_weights(p):
                sp.wait(*wr_free)
                got = wr_in.start(sp, raw_wr[:], wqrt[:, p * P:(p + 1) * P])
                dst = wr_slots[p % 2]
                act.wait(got, *wr_read[p % 2])
                hi = act.do(lambda q: q.activation(dst[:, 0], raw_wr[:], ACT.Copy))
                dve.wait(hi)
                lo = dve.do(lambda q: q.tensor_tensor(dst[:, 1], raw_wr[:], dst[:, 0].bitcast(F32), ALU.subtract))
                wr_free[:] = [lo]
                W[p, "wr"] = lo

            wr_free, wr_read = [], {0: [], 1: []}

            def rotate(p, b):
                toks = slice(b * SEQ, (b + 1) * SEQ)
                w = wr_slots[p % 2]
                bank = bank_ring.next()
                pe.wait(W[p, "wr"], *bank.free)
                done = product(pe, bank.ap, split3(w[:, 0], w[:, 1], cq[:, 0, toks], cq[:, 1, toks]))
                wr_read[p % 2] = [done]
                dve.wait(cos_here, done, *rotary.free)
                cosine = dve.do(lambda q: q.tensor_tensor(rot[:], bank.ap, cos_t[:], ALU.mult))
                act.wait(cosine, *rotary.free)
                for f in range(0, P, DR):
                    a, b, c = f, f + DR // 2, f + DR
                    act.do(lambda q, a=a, b=b, c=c: q.activation(rot_sin[a:b, :], bank.ap[b:c, :], ACT.Copy))
                    swapped = act.do(lambda q, a=a, b=b, c=c: q.activation(rot_sin[b:c, :], bank.ap[a:b, :], ACT.Copy))
                bank.free = [swapped]
                pool.wait(sin_here, swapped)
                sine = pool.do(lambda q: q.tensor_tensor(rot_sin[:], rot_sin[:], sin_t[:], ALU.mult))
                pool.wait(cosine, sine)
                turned = pool.do(lambda q: q.tensor_tensor(rot[:], rot[:], rot_sin[:], ALU.add))
                return turned

            def rotate_high(turned):
                up, dn = slice(0, DR), slice(DR, P)
                act.wait(turned, *qr.free)
                act.do(lambda q: q.activation(qr.ap[up, 0, :], rot[up, :], ACT.Copy))
                act.do(lambda q: q.activation(qr.ap[dn, 1, :], rot[dn, :], ACT.Copy))
                hi = act.do(lambda q: q.activation(qr.ap[up, 1, :], rot[dn, :], ACT.Copy))
                dve.wait(hi)
                dve.do(lambda q: q.tensor_tensor(qr.ap[dn, 0, :], rot[up, :], qr.ap[up, 0, :].bitcast(F32),
                                                 ALU.subtract))
                lo = dve.do(lambda q: q.tensor_tensor(qr.ap[dn, 1, :], rot[dn, :], qr.ap[dn, 1, :].bitcast(F32),
                                                      ALU.subtract))
                rotary.free = [lo]
                qr.ready = [lo]

            def queries(p, b):
                toks = slice(b * SEQ, (b + 1) * SEQ)
                m = m_slots[p % 2]
                act_wait = list(qc.free)
                rounded = []
                for h in range(2):
                    bank = bank_ring.next()
                    pe.wait(W[p, h][0], *bank.free)
                    done = product(pe, bank.ap, split3(m[:, h, 0, :], m[:, h, 1, :], cq[:, 0, toks], cq[:, 1, toks]))
                    act.wait(*act_wait)
                    act.wait(done)
                    rounded.append((bank, act.do(lambda q, h=h, bank=bank: q.activation(
                        qc.ap[:, 0, h, :], bank.ap, ACT.Copy))))
                return rounded

            def queries_low(rounded):
                for h, (bank, hi) in enumerate(rounded):
                    dve.wait(hi)
                    lo = dve.do(lambda q, h=h, bank=bank: q.tensor_tensor(
                        qc.ap[:, 1, h, :], bank.ap, qc.ap[:, 0, h, :].bitcast(F32), ALU.subtract))
                    bank.free = [lo]
                qc.ready = [lo]

            def scores(b):
                pe.wait(*qc.ready)
                weights, low = [], []

                def take_low(g):
                    w, hi = weights[g][0], weights[g][1]
                    eng = pool if g == 0 else dve
                    eng.wait(hi, *pl_slots[g].free)
                    low.append(eng.do(lambda q: q.tensor_tensor(
                        pl_slots[g].ap, w.ap, ph_slots[g].ap.bitcast(F32), ALU.subtract)))

                for g, pieces in enumerate(GROUPS):
                    bank, w, ph = bank_ring.next(), p_ring.next(), ph_slots[g]
                    pe.wait(*bank.free)
                    off = 0
                    for k, q0, n in pieces:
                        keys = slice(b * SEQ + k * P, b * SEQ + (k + 1) * P)
                        toks = slice(q0, q0 + n)
                        pairs = split3(ckvt[:, 0, keys], ckvt[:, 1, keys], qc.ap[:, 0, :, toks], qc.ap[:, 1, :, toks])
                        part = bank.ap[:, off:off + 2 * n].rearrange("p (h t) -> p h t", h=2)
                        product(pe, part, pairs, last=False)
                        pe.wait(*qr.ready)
                        pairs = [(krot[:, 0, keys], qr.ap[:, :, toks]), (krot[:, 1, keys], qr.ap[:, :, toks])]
                        done = product(pe, part, pairs, first=False)
                        off += 2 * n
                    act.wait(done, *w.free)
                    exps = act.do(lambda q, w=w, bank=bank: q.activation(w.ap, bank.ap, ACT.Exp, scale=SCALE))
                    bank.free = [exps]
                    if g >= 1:
                        round_high(g - 1, weights)
                    dve.wait(exps)
                    ready = dve.do(lambda q, w=w: q.tensor_scalar(
                        w.ap, w.ap, float(np.exp(-CLIP * SCALE)), float(np.exp(CLIP * SCALE)), ALU.max, ALU.min))
                    if g in (0, 2, 4):
                        pool.wait(ready)
                        part = (w.ap.rearrange("p (h t) -> p h t", t=P) if g == 2
                                else w.ap.rearrange("p (h t) -> p h t", h=2)[:, :, 0:P])
                        ready = pool.do(lambda q, part=part, n=4 if g == 2 else 2: q.affine_select(
                            out=part, in_=part, compare_op=ALU.is_ge, fill=0.0, base=0,
                            pattern=[[0, n], [1, P]], channel_multiplier=-1))
                    weights.append([w, ready])
                    if g >= 2:
                        take_low(g - 2)
                take_low(NG - 2)
                qc.free = qr.free = [done]
                round_high(NG - 1, weights)
                return weights, low, take_low

            masked_at = {}

            def round_high(g, weights):
                w, ready = weights[g]
                act.wait(ready, *ph_slots[g].free)
                masked_at[g] = ready
                weights[g][1] = act.do(lambda q: q.activation(ph_slots[g].ap, w.ap, ACT.Copy))

            def add_up(weights):
                w = [x[0].ap.rearrange("p (h t) -> p h t", h=2) for x in weights]
                w1_q1 = weights[2][0].ap[:, 0:2 * P].rearrange("p (h t) -> p h t", h=2)
                w3_q3 = weights[2][0].ap[:, 2 * P:4 * P].rearrange("p (h t) -> p h t", h=2)
                pool.wait(masked_at[0], masked_at[1], masked_at[2], masked_at[3], masked_at[4], *sums.free)
                a_ready = pool.do(lambda q: q.tensor_tensor(sum_a[:], w[0][:, :, P:2 * P], w1_q1, ALU.add))
                t = pool.do(lambda q: q.tensor_tensor(sum_b[:], w[1], w[3], ALU.add))
                pool.wait(t)
                t = pool.do(lambda q: q.tensor_tensor(sum_b[:], sum_b[:], w[4], ALU.add))
                pool.wait(t)
                b_ready = pool.do(lambda q: q.tensor_tensor(sum_b[:, :, P:2 * P], sum_b[:, :, P:2 * P], w3_q3, ALU.add))
                for x, _ in weights:
                    x.free = [b_ready]
                return a_ready, b_ready

            def split_sums(a_ready, b_ready):
                act.wait(a_ready)
                a_hi = act.do(lambda q: q.activation(sum_a_hi[:], sum_a[:], ACT.Copy))
                act.wait(b_ready)
                b_hi = act.do(lambda q: q.activation(sum_b_hi, sum_b[:], ACT.Copy))
                pool.wait(a_hi)
                pool.do(lambda q: q.tensor_tensor(sum_a_lo[:], sum_a[:], sum_a_hi[:].bitcast(F32),
                                                  ALU.subtract))
                pool.wait(b_hi)
                return pool.do(lambda q: q.tensor_tensor(sum_b_lo, sum_b[:], sum_b_hi.bitcast(F32),
                                                         ALU.subtract))

            def attend(b, weights, low, split):
                whole_bank, second = (0, H2), (P, H2)
                plan = [[(0, 0, 0, whole_bank), (2, 0, 1, second)],
                        [(1, 0, 0, whole_bank), (3, 0, 1, whole_bank), (4, 0, 2, whole_bank), (2, 2 * P, 3, second)]]
                reads = []
                for n, steps in enumerate(plan):
                    bank = o_banks[n]
                    pe.wait(*bank.free)
                    for j, (g, a, k, (c0, c1)) in enumerate(steps):
                        t = b * TB + k
                        width = c1 - c0
                        pe.wait(low[g])
                        dst = bank.ap.rearrange("p (h t) -> p h t", h=2)[:, :, c0:c1]
                        hi, lo = (s[g].ap[:, a:a + 2 * width].rearrange("p (h t) -> p h t", h=2)
                                  for s in (ph_slots, pl_slots))
                        done = product(pe, dst, split3(ckv[:, 0, t, :], ckv[:, 1, t, :], hi, lo),
                                       first=j == 0, last=j == len(steps) - 1)
                    reads.append(done)
                bank, inv = bank_ring.next(), inv_ring.next()
                pe.wait(split, unit_rounded, *bank.free)
                row = bank.ap[0:2, :].rearrange("p (h t) -> p h t", h=2)
                first = [x[0].ap.rearrange("p (h t) -> p h t", h=2)[:, :, 0:P] for x in (ph_slots, pl_slots)]
                product(pe, row[:, :, 0:P], [(unit_r[:, 0, :], x) for x in first], last=False)
                product(pe, row[:, :, P:2 * P], [(unit_r[:, 0, :], sum_a_hi[:]),
                                                 (unit_r[:, 0, :], sum_a_lo[:])], first=False, last=False)
                dens = product(pe, row, [(unit_r[:, 1, :], sum_b_hi),
                                         (unit_r[:, 1, :], sum_b_lo)], first=False)
                for s in ph_slots + pl_slots:
                    s.free = [dens]
                sums.free = [dens]
                for x, _ in weights:
                    x.free += low
                o_ready = []
                for n in range(2):
                    act.wait(*o_slot.free)
                    o_ready.append(split_bank(reads[n], o_banks[n], o_slot.ap[:, 0, n], o_slot.ap[:, 1, n],
                                              o_banks[n].ap.rearrange("p (h t) -> p h t", h=2)))
                act.wait(dens, *rows_sent)
                in_rows = act.do(lambda q: q.activation(
                    divisor_rows[:].rearrange("s (p c) -> s c p", p=P),
                    bank.ap[0:2, :].rearrange("s (c p) -> s c p", p=P), ACT.Copy))
                bank.free = [in_rows]
                sp.wait(in_rows, *inv.free)
                n = inv_ring.at % 2
                rows_sent[:] = [divisor_sent[2 * s + n].start(
                    sp, inv.ap[:, s * TB:(s + 1) * TB], divisor_rows[s:s + 1, :].rearrange("o (p c) -> o p c", p=P))
                    for s in range(2)]
                return o_ready, inv, list(rows_sent)

            rows_sent = []

            def output(p, b, o_ready, inv, divisors, between=()):
                between = dict(between)
                dve.wait(*divisors)
                inverted = dve.do(lambda q: q.reciprocal(inv.ap, inv.ap))
                v = v_slots[p % 2]
                for tt in range(TB):
                    for h in range(2):
                        y = bank_ring.next()
                        n, c0 = tt // 2, tt % 2 * P
                        o = o_slot.ap[:, :, n, h, c0:c0 + P]
                        pe.wait(o_ready[n], W[p, h][1], *y.free)
                        done = product(pe, y.ap, split3(o[:, 0], o[:, 1], v[:, h, 0, :], v[:, h, 1, :]))
                        t = b * TB + tt
                        dve.wait(done, inverted, acc_done.get(t))
                        y_read = dve.do(lambda q, y=y, t=t, c=tt // 2 * TB + 2 * h + tt % 2: q.scalar_tensor_tensor(
                            acc[:, t, :], y.ap, inv.ap[:, c:c + 1], acc[:, t, :], ALU.mult, ALU.add))
                        y.free = [y_read]
                        acc_done[t] = y_read
                        if 2 * tt + h in between:
                            between[2 * tt + h]()
                    if p == PAIRS - 1:
                        sp.wait(y_read)
                        sent.append(out_sem[t].start(sp, out_t[:, t, :], acc[:, t, :]))
                o_slot.free = [done]
                inv.free = [y_read]

            sent = []
            units = [(p, b) for p in range(PAIRS) for b in range(NB)]
            act.wait(unit_made)
            unit_rounded = act.do(lambda q: q.activation(unit_r[:], unit[:], ACT.Copy))
            held = None
            for t in range(NT):
                now = project(t)
                if held:
                    turn(*held)
                held = now
                if t == TB + 2:
                    rotary_weights(0)
                if t == 2 * TB + 2:
                    turned = rotate(0, 0)
            xnt_read = Ticket(pe.sem, now[3])
            for queue in (act, dve, pool):
                queue.wait(xnt_read)
            rotate_high(turned)
            head_weights(0, 0)
            head_weights(0, 1)
            turn(*held)
            for s in p_ring.slots:
                s.free = all_done()
            queries_low(queries(0, 0))
            before = None
            for i, (p, b) in enumerate(units):
                after = units[i + 1] if i + 1 < len(units) else None
                weights, low, take_low = scores(b)
                summed = add_up(weights)
                if after:
                    rounded = queries(*after)
                    turned = rotate(*after)
                    queries_low(rounded)
                split = split_sums(*summed)
                rest = [(3, lambda: take_low(NG - 1))]
                if after:
                    rest.append((6, lambda: rotate_high(turned)))
                if before:
                    output(*before, between=rest)
                else:
                    for _, step in rest:
                        step()
                if b == 1 and p + 1 < PAIRS:
                    rotary_weights(p + 1)
                    head_weights(p + 1, 0)
                if b == 2 and p + 1 < PAIRS:
                    head_weights(p + 1, 1)
                before = (p, b, *attend(b, weights, low, split))
            output(*before)
            sp.wait(*sent)

            with nc.Block() as block:
                block.sync(lambda eng: sp.run(eng))
                block.gpsimd(lambda eng: pool.run(eng))
                block.scalar(lambda eng: act.run(eng))
                block.vector(lambda eng: dve.run(eng))
                block.tensor(lambda eng: pe.run(eng))


def rope_tables(seq, width, tile):
    inv_freq = (np.float32(10000.0) ** (-np.arange(0, width, 2, dtype=np.float32) / np.float32(width)))
    ang = np.arange(seq, dtype=np.float32)[:, None] * inv_freq.astype(np.float32)[None, :]
    c, s = np.cos(ang).astype(np.float32), np.sin(ang).astype(np.float32)
    cos = np.concatenate([c, c, c, c], axis=1).reshape(seq // tile, tile, 2 * width)
    sin = np.concatenate([-s, s, -s, s], axis=1).reshape(seq // tile, tile, 2 * width)
    cos_t, sin_t = (v.reshape(seq, 2 * width).T for v in (cos, sin))
    return cos.transpose(1, 0, 2), sin.transpose(1, 0, 2), cos_t, sin_t


def kernel(**inputs):
    import concourse.bacc as bacc
    from concourse.bass_utils import run_bass_kernel_spmd

    att, ffn = "L0_attn_", "L0_ffn_"
    a = {n: np.asarray(v) for n, v in inputs.items()}
    d_rot = a[att + "W_KR"].shape[0]
    heads = a[att + "W_QR"].shape[0] // d_rot
    wqr = a[att + "W_QR"].reshape(heads, d_rot // 2, 2, -1).transpose(0, 2, 1, 3).reshape(heads * d_rot, -1)
    wkr = a[att + "W_KR"].reshape(d_rot // 2, 2, -1).transpose(1, 0, 2).reshape(d_rot, -1)
    cos, sin, cos_t, sin_t = rope_tables(a[att + "x"].shape[1], d_rot, 128)
    laid = {
        "x": a[att + "x"], "wdqt": a[att + "W_DQ"].T, "wuq": a[att + "W_UQ"], "wqrt": wqr.T,
        "wdkvt": a[att + "W_DKV"].T, "wuk": a[att + "W_UK"], "wuv": a[att + "W_UV"], "wkrt": wkr.T,
        "wot": a[att + "W_O"].T,
        "w1": a[ffn + "W1"], "wg": a[ffn + "Wg"], "w2": a[ffn + "W2"],
        "ws1": a[ffn + "Ws1"], "wsg": a[ffn + "Wsg"], "ws2": a[ffn + "Ws2"],
        "gate_w": a[ffn + "gate_w"], "gate_b": a[ffn + "gate_b"], "biases": a[ffn + "biases"],
        "rope_cos": cos, "rope_sin": sin, "rope_cos_t": cos_t, "rope_sin_t": sin_t,
    }
    nc = bacc.Bacc("TRN2", target_bir_lowering=False, num_devices=1)
    arrays, args = {}, []
    for name, v in laid.items():
        arrays[f"in_{name}"] = np.ascontiguousarray(v)
        args.append(nc.dram_tensor(f"in_{name}", v.shape, F32, kind="ExternalInput").ap())
    args.append(nc.dram_tensor("out_0", a[att + "x"].shape, F32, kind="ExternalOutput").ap())
    program(nc, *args)
    r = run_bass_kernel_spmd(nc, [arrays], core_ids=[0])
    return r.results[0]["out_0"]
```
